# Optimizing a Trainium2 kernel written in Bass

```python
import numpy as np
import jax
import jax.numpy as jnp

def _softmax(x, axis=-1):
    return jax.nn.softmax(x, axis=axis)

def _gelu(x):
    return jax.nn.gelu(x, approximate=True)

def _silu(x):
    return jax.nn.silu(x)

def _sigmoid(x):
    return jax.nn.sigmoid(x)

def _layernorm(x, axis=-1, eps=1e-05):
    m = jnp.mean(x, axis=axis, keepdims=True)
    v = jnp.var(x, axis=axis, keepdims=True)
    return (x - m) / jnp.sqrt(v + eps)

def _scatter_add(tgt, idx, src, axis=0):
    return tgt.at[idx].add(src)

def _segment_sum(src, seg, n):
    return jax.ops.segment_sum(src, seg, n)
kernel_name = 'mk_gnn_resnorm_d2_gnn_r32_89bc29'

def setup_inputs(seed: int=0):
    np.random.seed(seed)
    _w = jnp.asarray

    def _rec_inputs():
        import jax
        import jax.numpy as jnp
        _gk = jax.random.key(seed)
        x = -0.000202 + 1 * jax.random.normal(jax.random.fold_in(_gk, 1), (3125, 128), jnp.float32)
        _s = jax.random.randint(jax.random.fold_in(_gk, 2), (50000,), 0, 3125, jnp.int32)
        _d = jax.random.randint(jax.random.fold_in(_gk, 3), (50000,), 0, 3125, jnp.int32)
        _loop = jnp.arange(3125, dtype=jnp.int32)
        src = jnp.concatenate([_s, _d, _loop])
        dst = jnp.concatenate([_d, _s, _loop])
        _o = jnp.argsort(dst, stable=True)
        src = src[_o]
        dst = dst[_o]
        edge_attr_64 = -5.16925e-05 + 1.00005 * jax.random.normal(jax.random.fold_in(_gk, 11), (103125, 64), jnp.float32)
        return (x, src, dst, edge_attr_64)
    x, src, dst, edge_attr_64 = _rec_inputs()

    def _L0_gnn_setup():
        import jax, jax.numpy as jnp
        import numpy as np
        N_NODES = 50000
        N_EDGES = 25000
        D = 128

        def _sage_dir(x, W, b, src, dst, num_nodes):
            msgs = x[src]
            agg = jax.ops.segment_sum(msgs, dst, num_segments=num_nodes)
            deg = jax.ops.segment_sum(jnp.ones((src.shape[0],), x.dtype), dst, num_segments=num_nodes)
            mean = agg / jnp.maximum(deg, 1.0)[:, None]
            return mean @ W.T + b
        key = jax.random.key(seed)
        ks = jax.random.split(key, 6)
        scale = 1.0 / np.sqrt(D)
        x = jax.random.normal(ks[0], (N_NODES, D), dtype=jnp.float32)
        edge_index = jax.random.randint(ks[1], (2, N_EDGES), 0, N_NODES, dtype=jnp.int64)
        W_in = jax.random.normal(ks[2], (D, D), dtype=jnp.float32) * scale
        W_out = jax.random.normal(ks[3], (D, D), dtype=jnp.float32) * scale
        W_root = jax.random.normal(ks[4], (D, D), dtype=jnp.float32) * scale
        b = jnp.zeros((D,), jnp.float32)
        return {'x': x, 'edge_index': edge_index, 'W_in': W_in, 'b_in': b, 'W_out': W_out, 'b_out': b, 'W_root': W_root, 'b_root': b}
    _L0_gnn_all = _L0_gnn_setup()
    _L0_gnn_in = {k: v for k, v in _L0_gnn_all.items() if k in ('W_in', 'b_in', 'W_out', 'b_out', 'W_root', 'b_root')}
    del _L0_gnn_all

    def _L1_gnn_setup():
        import jax, jax.numpy as jnp
        import numpy as np
        NEG_SLOPE = 0.2
        key = jax.random.key(seed)
        ks = jax.random.split(key, 10)
        N, E, D, ED = (3125, 50000, 128, 64)
        x = jax.random.normal(ks[0], (N, D), dtype=jnp.float32)
        edge_index = jax.random.randint(ks[1], (2, E), 0, N, dtype=jnp.int32)
        edge_attr = jax.random.normal(ks[2], (E, ED), dtype=jnp.float32)
        s = 1.0 / np.sqrt(D)
        W = jax.random.normal(ks[3], (D, D), dtype=jnp.float32) * s
        att_src = jax.random.normal(ks[4], (D,), dtype=jnp.float32) * s
        att_dst = jax.random.normal(ks[5], (D,), dtype=jnp.float32) * s
        bias = jnp.zeros((D,), dtype=jnp.float32)
        We = jax.random.normal(ks[6], (ED, D), dtype=jnp.float32) / np.sqrt(ED)
        be = jnp.zeros((D,), dtype=jnp.float32)
        return {'x': x, 'edge_index': edge_index, 'edge_attr': edge_attr, 'W': W, 'att_src': att_src, 'att_dst': att_dst, 'bias': bias, 'We': We, 'be': be}
    _L1_gnn_all = _L1_gnn_setup()
    _L1_gnn_in = {k: v for k, v in _L1_gnn_all.items() if k in ('W', 'att_src', 'att_dst', 'bias', 'We', 'be')}
    del _L1_gnn_all
    return {'x': x, 'src': src, 'dst': dst, 'edge_attr_64': edge_attr_64, 'L0_gnn_W_in': _L0_gnn_in['W_in'], 'L0_gnn_b_in': _L0_gnn_in['b_in'], 'L0_gnn_W_out': _L0_gnn_in['W_out'], 'L0_gnn_b_out': _L0_gnn_in['b_out'], 'L0_gnn_W_root': _L0_gnn_in['W_root'], 'L0_gnn_b_root': _L0_gnn_in['b_root'], 'L1_gnn_W': _L1_gnn_in['W'], 'L1_gnn_att_src': _L1_gnn_in['att_src'], 'L1_gnn_att_dst': _L1_gnn_in['att_dst'], 'L1_gnn_bias': _L1_gnn_in['bias'], 'L1_gnn_We': _L1_gnn_in['We'], 'L1_gnn_be': _L1_gnn_in['be']}

def reference(x, src, dst, edge_attr_64, L0_gnn_W_in, L0_gnn_b_in, L0_gnn_W_out, L0_gnn_b_out, L0_gnn_W_root, L0_gnn_b_root, L1_gnn_W, L1_gnn_att_src, L1_gnn_att_dst, L1_gnn_bias, L1_gnn_We, L1_gnn_be):
    import jax
    import jax.numpy as jnp

    def _L0_gnn_ref(x, edge_index, W_in, b_in, W_out, b_out, W_root, b_root):
        import jax, jax.numpy as jnp
        import numpy as np
        N_NODES = 50000
        N_EDGES = 25000
        D = 128

        def _sage_dir(x, W, b, src, dst, num_nodes):
            msgs = x[src]
            agg = jax.ops.segment_sum(msgs, dst, num_segments=num_nodes)
            deg = jax.ops.segment_sum(jnp.ones((src.shape[0],), x.dtype), dst, num_segments=num_nodes)
            mean = agg / jnp.maximum(deg, 1.0)[:, None]
            return mean @ W.T + b
        alpha = 0.5
        src, dst = (edge_index[0], edge_index[1])
        n = x.shape[0]
        x_in = _sage_dir(x, W_in, b_in, src, dst, n)
        x_out = _sage_dir(x, W_out, b_out, dst, src, n)
        out = alpha * x_out + (1.0 - alpha) * x_in
        out = out + x @ W_root.T + b_root
        return out

    def _L1_gnn_ref(x, edge_index, edge_attr, W, att_src, att_dst, bias, We, be):
        import jax, jax.numpy as jnp
        import numpy as np
        NEG_SLOPE = 0.2
        N = x.shape[0]
        edge_feat = edge_attr @ We + be
        h = x @ W
        loop = jnp.arange(N, dtype=edge_index.dtype)
        src = jnp.concatenate([edge_index[0], loop])
        dst = jnp.concatenate([edge_index[1], loop])
        a_s = h @ att_src
        a_d = h @ att_dst
        e = jax.nn.leaky_relu(a_s[src] + a_d[dst], NEG_SLOPE)
        seg_max = jax.ops.segment_max(e, dst, num_segments=N)
        e = jnp.exp(e - seg_max[dst])
        denom = jax.ops.segment_sum(e, dst, num_segments=N)
        alpha = e / (denom[dst] + 1e-16)
        out = jax.ops.segment_sum(h[src] * alpha[:, None], dst, num_segments=N)
        return out + bias
    edge_index = jnp.stack([src, dst])
    x = _layernorm(x + _L0_gnn_ref(x, edge_index, L0_gnn_W_in, L0_gnn_b_in, L0_gnn_W_out, L0_gnn_b_out, L0_gnn_W_root, L0_gnn_b_root), axis=-1)
    x = _layernorm(x + _L1_gnn_ref(x, edge_index, edge_attr_64, L1_gnn_W, L1_gnn_att_src, L1_gnn_att_dst, L1_gnn_bias, L1_gnn_We, L1_gnn_be), axis=-1)
    return x

_drawn_inputs = setup_inputs


def setup_inputs(seed=0):
    import zlib

    import numpy as np

    out = dict(_drawn_inputs(seed))
    spreads = {'L0_gnn_b_in': (0.0, 0.1),
     'L0_gnn_b_out': (0.0, 0.1),
     'L0_gnn_b_root': (0.0, 0.1),
     'L1_gnn_bias': (0.0, 0.1),
     'L1_gnn_be': (0.0, 0.1)}
    factors = {}
    for name, (base, spread) in spreads.items():
        noise = np.random.default_rng([zlib.crc32(name.encode()), seed]).standard_normal(out[name].shape)
        drawn = base * np.exp(spread * noise) if base else spread * noise
        out[name] = jnp.asarray(drawn.astype(out[name].dtype))
    for name, factor in factors.items():
        out[name] = (out[name] * factor).astype(out[name].dtype)
    return out
```

```python
import concourse.bass as bass
from concourse import mybir
from contextlib import ExitStack


def gnn_resnorm_kernel(nc, x, src, dst, W_in, b_in, W_out, b_out, W_root, b_root,
                       W_gat, att_src, att_dst, b_gat, out):
    f32, bf16, i32 = mybir.dt.float32, mybir.dt.bfloat16, mybir.dt.int32
    ALU = mybir.AluOpType
    ACT = mybir.ActivationFunctionType
    AX = mybir.AxisListType.X

    N, D = x.shape
    E = src.shape[0]
    P = 125
    T = N // P
    EC = E // P
    WN = P // T
    NW = N // WN
    G = NW // P
    GW = P // WN // 5
    NG = 5
    CAP = 256
    HALVES = 2
    ALIGN = 32
    NR = E // ALIGN + 1
    PAD = (NR - 1) * ALIGN + CAP - E
    WSPAN = WN * N
    CH = 500
    CHUNKS = [(c, min(CH, N - c)) for c in range(0, N, CH)]
    NC = len(CHUNKS)
    CHUNK_AT = [[0, 1], [2, 3], [4], [5], [6]]
    PAIRS = 11
    GB = 15
    NB = EC // GB
    NEG = -1.0e30
    SLOPE = 0.2
    EPS = 1e-5
    CONSTS = 12
    TAIL_STEPS = 25
    assert T * P == N and P * EC == E and WN * T == P and NB * GB == EC

    flat_keys = nc.dram_tensor("flat_keys", [E + PAD], f32, kind="Internal").ap()
    key_rows = nc.dram_tensor("key_rows", [NR, CAP], f32, kind="Internal").ap()
    counts = nc.dram_tensor("counts", [N, N], f32, kind="Internal").ap()

    ctx = ExitStack()
    with ctx:
        def sb(name, shape, dt=f32):
            return ctx.enter_context(nc.sbuf_tensor(name, shape, dt))

        def sem(name):
            return ctx.enter_context(nc.semaphore(name))

        X = sb("X", [P, T, D])
        X1 = sb("X1", [P, T, D])
        H = sb("H", [P, T, D + 1])
        sums_in = sb("sums_in", [D, N])
        sums_out = sb("sums_out", [D, N])
        AT = [sb(f"AT{b}", [P, T, P]) for b in range(2)]
        AR = [sb(f"AR{b}", [P, N]) for b in range(2)]
        S = [sb(f"S{b}", [P, N]) for b in range(2)]
        xt = [sb(f"xt{b}", [P, D]) for b in range(2)]
        row_key = sb("row_key", [128, HALVES, NW], bf16)
        col_key = sb("col_key", [128, HALVES, NW], bf16)
        row_hot = sb("row_hot", [128, 2, GW, HALVES, P], bf16)
        col_hot = sb("col_hot", [128, 2, GW, HALVES, P], bf16)
        all_row = sb("all_row", [P, EC])
        all_col = sb("all_col", [P, EC])
        iota_b = sb("iota_b", [128, P], bf16)
        iota_f = sb("iota_f", [128, P])
        iota_i = sb("iota_i", [128, P], i32)
        window_i = sb("window_i", [P, G], i32)
        window = sb("window", [P, G])
        ident = sb("ident", [128, 128])
        ones = sb("ones", [P, P])
        ones_row = sb("ones_row", [1, P])
        WiT = sb("WiT", [D, D])
        WoT = sb("WoT", [D, D])
        WrT = sb("WrT", [D, D])
        Wg = sb("Wg", [D, D])
        rows_in = sb("rows_in", [1, 6, D])
        brow = sb("brow", [1, 4, D])
        bc = sb("bc", [P, 4, D])
        x5 = sb("x5", [P, 5, D])
        x5T = sb("x5T", [D, 5, P])
        si5 = sb("si5", [D, 5, P])
        so5 = sb("so5", [D, 5, P])
        y5 = sb("y5", [P, 5, D])
        t5 = sb("t5", [P, 5, D])
        PT = [sb(f"PT{b}", [P, 5, P]) for b in range(2)]
        deg_part = sb("deg_part", [P, T * NG])
        deg_in = sb("deg_in", [P, T])
        deg_out = sb("deg_out", [P, T])
        a_s = sb("a_s", [P, T])
        a_d = sb("a_d", [P, T])
        st6 = sb("st6", [P, 5, 6])
        mv = sb("mv", [P, 5, 2])
        rstd = sb("rstd", [P, 5])
        ve5 = sb("ve5", [P, 5])
        mhalf = sb("mhalf", [P, 5])
        mx = [sb(f"mx{b}", [P, 4]) for b in range(2)]
        fin = [sb(f"fin{b}", [P, D]) for b in range(2)]
        rden = [sb(f"rden{b}", [P, 1]) for b in range(2)]
        st2 = [sb(f"st2{b}", [P, 6]) for b in range(2)]
        mv2 = [sb(f"mv2{b}", [P, 2]) for b in range(2)]
        ve2 = [sb(f"ve2{b}", [P, 1]) for b in range(2)]
        rs2 = [sb(f"rs2{b}", [P, 1]) for b in range(2)]
        diag = [so5, si5]
        total = sb("total", [1, 1])
        tick = sb("tick", [1, 8])
        tick_pool = sb("tick_pool", [1, 2])
        flag = sb("flag", [1, 1], i32)
        R = [AT[b][:, :, :].rearrange("p a b -> p (a b)") for b in range(2)]
        deg_sum = X1[:, :, 0:P]
        a_row = sums_out
        dst_i = S[0][:, 0:EC].bitcast(i32)
        src_i = S[0][:, EC:2 * EC].bitcast(i32)
        flat = S[0][:, 2 * EC:3 * EC]
        q_i = AR[1][:, 0:G * CAP].bitcast(i32)
        q_f = AR[1][:, G * CAP:2 * G * CAP]
        neg_f = AT[0][:, :, :].rearrange("p a b -> p (a b)")[:, 0:G * CAP]
        rem_f = AT[1][:, :, :].rearrange("p a b -> p (a b)")[:, 0:G * CAP]
        win = AT[1][:, :, :].rearrange("p a b -> p (a b)")[:, G * CAP:2 * G * CAP]
        cand = S[1][:, 0:EC].bitcast(i32)
        flat2 = sums_in[0:P, 0:EC]
        cmp_f = S[1][:, EC:2 * EC]
        heads = AR[0][:, 128:128 + P]
        pad = S[1][0:1, 2 * EC:2 * EC + PAD]
        wbase = AR[0][:, 0:G]
        krow = AR[0][:, 8:8 + G]
        rowno = AR[0][:, 16:16 + G]
        start = AR[0][:, 24:24 + G]
        rowno_i = AR[0][:, 32:32 + G].bitcast(i32)
        start_i = AR[0][:, 40:40 + G].bitcast(i32)
        c2 = AR[0][:, 48:48 + G]
        okc = AR[0][:, 56:57]
        Wst = [sb(f"Wst{k}", [D, D]) for k in range(3)]
        gen_row = S[0][:, 0:GB * P].rearrange("p (c k) -> p c k", c=GB)
        gen_col = S[1][:, 0:GB * P].rearrange("p (c k) -> p c k", c=GB)
        gen_key = S[0][:, GB * P:GB * P + EC]
        zero_w = sb("zero_w", [P, P])
        win_off = sb("win_off", [P, NW])
        win_off_i = S[1][:, 3 * EC:3 * EC + NW].bitcast(i32)

        bank = [ctx.enter_context(nc.psum_tensor(f"bank{k}", [128, 1024], f32)) for k in range(4)]
        BP, TP = bank[0], bank[1]
        OP = [bank[2][:, 0:512], bank[2][:, 512:1024]]
        AI = bank[3][:, 0:512]
        OPX = bank[3][0:1, 512:513]

        def slots(b, rows, n=5, w=P):
            return b[0:rows, 0:n * 128].rearrange("p (k j) -> p k j", j=128)[:, :, 0:w]

        s_ld = {k: sem("loaded_" + k) for k in ("dst", "src", "w", "rows", "x")}
        s_xt = [sem("xt_loaded0"), sem("xt_loaded1")]
        s_const = sem("constants_made")
        s_chain = sem("prelude_vector_step")
        s_hb0 = sem("heads_converted")
        s_brow = sem("constant_rows_made")
        s_bc = sem("constant_rows_spread")
        s_bcs = sem("constant_rows_saved")
        s_f2 = sem("layer2_finish_step")
        s_wt = sem("weights_transposed_L1")
        s_wts = sem("weights_saved")
        s_hb = sem("heads_on_every_row")
        s_flatk = sem("flat_keys_made")
        s_flat = sem("flat_keys_stored")
        s_rows = sem("key_rows_stored")
        s_rowno = sem("candidate_rows_known")
        s_cand = sem("candidate_row_loaded")
        s_candused = sem("candidate_row_used")
        s_start = sem("window_starts_known")
        s_win = sem("windows_loaded")
        s_wkeys = sem("window_keys_made")
        s_wkt = sem("window_keys_transposed")
        s_wks = sem("window_keys_saved")
        s_vsum = sem("valid_edges_counted")
        s_vtot = sem("valid_edges_summed")
        s_flag = sem("flag_known")
        s_hot = sem("onehots_ready")
        s_gkey = sem("general_keys_ready")
        s_ghot = sem("general_onehots_ready")
        s_ghotused = sem("general_onehots_used")
        s_built = sem("window_counts_built")
        s_at = sem("AT_group_ready")
        s_tp = sem("AR_group_transposed")
        s_ar = sem("AR_group_ready")
        s_ai = sem("sums_in_tile_done")
        s_agin = sem("sums_in_tile_saved")
        s_out = sem("sums_out_chunk_done")
        s_acc = sem("sums_out_chunk_added")
        s_deg = sem("degree_added")
        s_store = [sem("counts_stored0"), sem("counts_stored1")]
        s_x5 = sem("tail_x_ready")
        s_si5 = sem("tail_sums_in_ready")
        s_so5 = sem("tail_sums_out_ready")
        s_x5T = sem("tail_xT_transposed")
        s_x5Ts = sem("tail_xT_saved")
        s_o5 = sem("tail_products_done")
        s_ve5 = sem("tail_variance")
        s_rs5 = sem("tail_rstd")
        s_y5 = sem("tail_normalized")
        s_y5T = sem("tail_yT_transposed")
        s_y5Ts = sem("tail_yT_saved")
        s_h5 = sem("tail_h_done")
        s_h5s = sem("tail_h_saved")
        s_tail = sem("tail_vector_step")
        s_tdone = sem("tail_batch_done")
        s_diag = sem("a_s_diagonal_ready")
        s_arow = sem("a_s_row_done")
        s_arows = sem("a_s_row_saved")
        s_load = [sem("counts_loaded0"), sem("counts_loaded1")]
        s_self = sem("self_loops_added")
        s_pen = sem("mask_ready")
        s_m = sem("max_ready")
        s_relu = sem("relu_done")
        s_lr = sem("leaky_done")
        s_e = sem("exp_done")
        s_p = sem("weights_ready")
        s_t2 = sem("weights_transposed")
        s_eva = sem("PT_saved_by_scalar")
        s_evd = sem("PT_saved_by_vector")
        s_mm = sem("PT_used")
        s_c2 = sem("layer2_vector_step")
        s_ve2 = sem("layer2_variance")
        s_rs2 = sem("layer2_rstd")
        s_fin = sem("row_tile_ready")
        s_res = [sem("result_stored0"), sem("result_stored1")]

        def ge(eng, s, v):
            if not isinstance(v, int) or v > 0:
                eng.wait_ge(s, v)

        def carry(i):
            nc.vector.memset(tick[:, i:i + 1], 0.0)

        class Chain:
            def __init__(self, eng, s, base=0):
                self.eng, self.s, self.base, self.n = eng, s, base, 0

            def add(self, ins):
                ins.then_inc(self.s, 1)
                self.n += 1

            def wait(self):
                self.eng.wait_ge(self.s, self.base + self.n)

            def __call__(self, ins):
                self.add(ins)
                self.wait()

        def steps(eng, body, last):
            for t in range(4):
                body(t // 2, t % 2, t)
            with eng.Fori(2, PAIRS) as k:
                for b in range(2):
                    body(k, b, 2 * k + b)
            for t in range(2 * PAIRS, last + 1):
                body(t // 2, t % 2, t)

        def has(t, lo=0):
            return not isinstance(t, int) or lo <= t < T

        def cols(t, w):
            return slice(t * w, (t + 1) * w) if isinstance(t, int) else bass.ds(t * w, w)

        block = ctx.enter_context(nc.Block())
        xv = x.rearrange("(t p) d -> p t d", p=P)

        @block.sync
        def _(sp):
            sp.dma_start(dst_i, dst.rearrange("(p c) -> p c", c=EC)).then_inc(s_ld["dst"], 16)
            sp.dma_start(src_i, src.rearrange("(p c) -> p c", c=EC)).then_inc(s_ld["src"], 16)
            for k, w in enumerate((W_in, W_out, W_root)):
                sp.dma_start(Wst[k][:, :], w).then_inc(s_ld["w"], 16)
            sp.dma_start(Wg[:, :], W_gat).then_inc(s_ld["w"], 16)
            for k, r in enumerate((att_src, att_dst, b_gat, b_in, b_out, b_root)):
                sp.dma_start(rows_in[:, k, :], r.rearrange("(a d) -> a d", a=1)).then_inc(s_ld["rows"], 16)
            sp.dma_start(X[:, :, :], xv).then_inc(s_ld["x"], 16)
            sp.wait_ge(s_flatk, 1)
            sp.dma_start(flat_keys[0:E].rearrange("(p c) -> p c", c=EC), flat).then_inc(s_flat, 16)
            sp.wait_ge(s_const, CONSTS)
            sp.dma_start(flat_keys[E:E + PAD].rearrange("(a c) -> a c", a=1), pad).then_inc(s_flat, 16)
            sp.wait_ge(s_flat, 32)
            overlapping = bass.AP(flat_keys.tensor, 0, [[ALIGN, NR], [1, CAP]])
            sp.dma_start(key_rows, overlapping).then_inc(s_rows, 16)

            def step(k, b, t):
                if has(t):
                    ge(sp, s_out, NC * (t - 1))
                    sp.dma_start(xt[b][:, :], x[cols(t, P), :]).then_inc(s_xt[b], 16)
                if has(t - 1):
                    ge(sp, s_ar, NG * t)
                    sp.dma_start(counts[cols(t - 1, P), :], AR[1 - b][:, :]).then_inc(s_store[1 - b], 16)
            steps(sp, step, T)
            sp.wait_ge(s_store[0], 16 * 13)
            sp.wait_ge(s_store[1], 16 * 12)
            sp.wait_ge(s_out, NC * T)

            sp.dma_start(AR[0][:, :], counts[cols(0, P), :]).then_inc(s_load[0], 16)

            def step2(k, b, t):
                if has(t + 1):
                    ge(sp, s_p, t)
                    sp.dma_start(AR[1 - b][:, :], counts[cols(t + 1, P), :]).then_inc(s_load[1 - b], 16)
                if has(t - 2):
                    ge(sp, s_fin, t - 1)
                    sp.dma_start(out[cols(t - 2, P), :], fin[b][:, :]).then_inc(s_res[b], 16)
            steps(sp, step2, T + 1)
            sp.wait_ge(s_res[0], 16 * 13)
            sp.wait_ge(s_res[1], 16 * 12)

        @block.gpsimd
        def _(pool):
            pool.memset(ident[:, :], 0.0).then_inc(s_const, 1)
            pool.wait_ge(s_const, 1)
            pool.affine_select(out=ident[:, :], in_=ident[:, :], compare_op=ALU.not_equal, fill=1.0,
                               base=0, pattern=[[-1, 128]], channel_multiplier=1).then_inc(s_const, 1)
            pool.iota(iota_i[:, :], pattern=[[1, P]], base=0, channel_multiplier=0).then_inc(s_const, 1)
            pool.iota(window_i[:, :], pattern=[[P, G]], base=0, channel_multiplier=1).then_inc(s_const, 1)
            pool.iota(win_off_i, pattern=[[P, NW]], base=0, channel_multiplier=0).then_inc(s_const, 1)
            for tile, v in ((ones[:, :], 1.0), (ones_row[:, :], 1.0), (pad, -1.0e6), (zero_w[:, :], 0.0),
                            (mhalf[:, :], -0.5), (H[:, :, D:D + 1], 1.0), (deg_sum, 0.0)):
                pool.memset(tile, v).then_inc(s_const, 1)
            pool.wait_ge(s_rowno, 1)
            for g in range(G):
                if g:
                    pool.wait_ge(s_candused, g)
                pool.indirect_dma_start(cand, None, dst.rearrange("(p c) -> p c", c=EC),
                                        bass.IndirectOffsetOnAxis(ap=rowno_i[:, g:g + 1], axis=0)
                                        ).then_inc(s_cand, 16)
            pool.wait_ge(s_start, 1)
            pool.wait_ge(s_rows, 16)
            for g in range(G):
                pool.indirect_dma_start(win[:, g * CAP:(g + 1) * CAP], None, key_rows,
                                        bass.IndirectOffsetOnAxis(ap=start_i[:, g:g + 1], axis=0)
                                        ).then_inc(s_win, 16)

            def step(k, b, t):
                if not has(t - 1):
                    return
                ge(pool, s_at, NG * t)
                ge(pool, s_deg, t - 1)
                pool.tensor_tensor(deg_sum, deg_sum, AT[1 - b][:, :, :], ALU.add).then_inc(s_deg, 1)
            steps(pool, step, T)

            with pool.Fori(0, T // 5) as j:
                pool.wait_ge(s_ve5, j + 1)
                pool.tensor_tensor(rstd[:, :], ve5[:, :], mhalf[:, 0:5], ALU.pow).then_inc(s_rs5, 1)

            pool.wait_ge(s_arows, NC)

            def step2(k, b, t):
                if has(t):
                    ge(pool, s_self, t + 1)
                    ge(pool, s_t2, NG * (t - 1))
                    pool.tensor_tensor(tick_pool[:, b:b + 1], zero_w[0:1, 0:1], zero_w[0:1, 0:1], ALU.mult)
                    pool.tensor_scalar(S[b][:, :], AR[b][:, :], 0.0, NEG, ALU.is_equal, ALU.mult
                                       ).then_inc(s_pen, 1)
                if has(t - 2):
                    ge(pool, s_ve2, t - 1)
                    pool.tensor_tensor(rs2[b][:, :], ve2[b][:, :], mhalf[:, 0:1], ALU.pow).then_inc(s_rs2, 1)
            steps(pool, step2, T + 1)

        @block.scalar
        def _(act):
            act.wait_ge(s_wt, 1)
            for k, (w, f) in enumerate(((WiT, 0.5), (WoT, 0.5), (WrT, 1.0))):
                act.activation(w[:, :], AI[:, k * D:(k + 1) * D], ACT.Copy, scale=f).then_inc(s_wts, 1)
            act.wait_ge(s_flag, 1)

            def step(k, b, t):
                for g in range(NG):
                    if has(t):
                        if g == 0:
                            ge(act, s_ai, t - 1)
                            ge(act, s_deg, t - 1)
                        ge(act, s_built, NG * t + g + 1)
                        act.activation(AT[b][:, :, g * GW * WN:(g + 1) * GW * WN].rearrange("p h (w l) -> p w l h", l=WN),
                                       slots(BP, P).rearrange("p w (l h) -> p w l h", h=T), ACT.Copy
                                       ).then_inc(s_at, 1)
                    if has(t - 1):
                        if g == 0:
                            ge(act, s_out, NC * (t - 2))
                            ge(act, s_store[1 - b], 16 * (k - 1 + b))
                        ge(act, s_tp, NG * (t - 1) + g + 1)
                        act.activation(AR[1 - b][:, g * 625:(g + 1) * 625].rearrange("p (k j) -> p k j", k=5),
                                       slots(TP, P), ACT.Copy, accum_out=deg_part[:, cols((t - 1) * NG + g, 1)]
                                       ).then_inc(s_ar, 1)
                if has(t - 1):
                    ge(act, s_ai, t)
                    act.activation(sums_in[:, cols(t - 1, P)], AI[:, 0:P], ACT.Copy).then_inc(s_agin, 1)
            steps(act, step, T)

            act.wait_ge(s_ld["x"], 16)
            act.wait_ge(s_agin, T)
            with act.Fori(0, T // 5) as j:
                act.wait_ge(s_tdone, j + 1)
                act.activation(x5[:, :, :], X[:, bass.ds(5 * j, 5), :], ACT.Copy).then_inc(s_x5, 1)
                act.activation(si5[:, :, :].rearrange("p a b -> p (a b)"), sums_in[:, bass.ds(5 * P * j, 5 * P)],
                               ACT.Copy).then_inc(s_si5, 1)
                act.wait_ge(s_x5T, j + 1)
                act.activation(x5T[:, :, :], slots(bank[3], D), ACT.Copy).then_inc(s_x5Ts, 1)
                act.wait_ge(s_y5T, j + 1)
                act.activation(x5T[:, :, :], slots(bank[3], D), ACT.Copy).then_inc(s_y5Ts, 1)
                act.wait_ge(s_h5, j + 1)
                act.activation(H[:, bass.ds(5 * j, 5), 0:D], slots(bank[0], P, w=D), ACT.Copy).then_inc(s_h5s, 1)

            def scores(t, b):
                act.wait_ge(s_m, t + 1)
                act.activation(R[b], S[b][:, :], ACT.Relu, bias=mx[b][:, 3:4]).then_inc(s_relu, 1)
                act.wait_ge(s_lr, t + 1)
                act.activation(S[b][:, :], S[b][:, :], ACT.Exp, bias=mx[b][:, 2:3], scale=1.0 - SLOPE).then_inc(s_e, 1)

            def evict(t, b, g):
                act.wait_ge(s_t2, NG * t + g + 1)
                ge(act, s_mm, NG * t + g - 1)
                q = (b + g) % 2
                act.activation(PT[q][:, :, :], slots(bank[q], P), ACT.Copy).then_inc(s_eva, 1)

            scores(0, 0)

            def step2(k, b, t):
                evict(t, b, 0)
                evict(t, b, 1)
                if has(t + 1):
                    scores(t + 1, 1 - b)
                evict(t, b, 4)
            steps(act, step2, T - 1)

        @block.vector
        def _(dve):
            chain = Chain(dve, s_chain)
            V = nc.vector

            def floor_div(value, q_out, rem_out, qi, neg):
                chain(V.tensor_scalar(qi, value, 0.5, 1.0 / P, ALU.add, ALU.mult))
                chain(V.tensor_copy(q_out, qi))
                chain(V.scalar_tensor_tensor(out=rem_out, in0=q_out, scalar=-float(P), in1=value,
                                             op0=ALU.mult, op1=ALU.add))
                chain(V.tensor_scalar(neg, rem_out, 0.0, None, ALU.is_lt))
                chain(V.tensor_tensor(q_out, q_out, neg, ALU.subtract))
                chain(V.scalar_tensor_tensor(out=rem_out, in0=neg, scalar=float(P), in1=rem_out,
                                             op0=ALU.mult, op1=ALU.add))

            dve.wait_ge(s_const, CONSTS)
            chain(V.tensor_copy(window[:, :], window_i[:, :]))
            chain(V.tensor_scalar(wbase, window[:, :], float(WN), None, ALU.mult))
            dve.wait_ge(s_ld["dst"], 16)
            chain(V.tensor_copy(cmp_f[:, 0:1], dst_i[:, 0:1]))
            V.tensor_scalar(heads, ident[0:P, 0:P], cmp_f[:, 0:1], None, ALU.mult).then_inc(s_hb0, 1)
            dve.wait_ge(s_ld["src"], 16)
            V.scalar_tensor_tensor(out=flat, in0=dst_i, scalar=float(N), in1=src_i,
                                   op0=ALU.mult, op1=ALU.add).then_inc(s_flatk, 1)
            dve.wait_ge(s_flatk, 1)
            dve.wait_ge(s_hb, 1)
            for g in range(G):
                chain(V.tensor_scalar(cmp_f[:, 0:P], AI[0:P, 0:P], wbase[:, g:g + 1], 0.0, ALU.is_lt, ALU.add,
                                      accum_out=krow[:, g:g + 1]))
            chain(V.tensor_scalar(rowno, krow, -1.0, 0.0, ALU.add, ALU.max))
            V.tensor_copy(rowno_i, rowno).then_inc(s_rowno, 1)
            chain(V.tensor_copy(flat2, src_i))
            floor_div(flat2, all_row[:, :], all_col[:, :], q_i[:, 0:EC], neg_f[:, 0:EC])
            chain(V.scalar_tensor_tensor(out=all_row[:, :], in0=dst_i, scalar=float(T), in1=all_row[:, :],
                                         op0=ALU.mult, op1=ALU.add))
            chain(V.tensor_copy(iota_b[:, :], iota_i[:, :]))
            chain(V.tensor_copy(iota_f[:, :], iota_i[:, :]))
            chain(V.tensor_copy(win_off[:, :], win_off_i))
            for g in range(G):
                dve.wait_ge(s_cand, 16 * (g + 1))
                V.tensor_scalar(cmp_f, cand, wbase[:, g:g + 1], 0.0, ALU.is_lt, ALU.add,
                                accum_out=krow[:, g:g + 1]).then_inc(s_candused, 1)
                dve.wait_ge(s_candused, g + 1)
            chain(V.scalar_tensor_tensor(out=start, in0=rowno, scalar=float(EC), in1=krow, op0=ALU.mult, op1=ALU.add))
            chain(V.tensor_copy(start_i, start))
            V.tensor_scalar(start_i, start_i, 5, None, ALU.arith_shift_right).then_inc(s_start, 1)
            dve.wait_ge(s_ld["rows"], 16 * 6)
            chain(V.tensor_copy(brow[:, 0:3, :], rows_in[:, 0:3, :]))
            chain(V.tensor_tensor(brow[:, 3, :], rows_in[:, 3, :], rows_in[:, 4, :], ALU.add))
            V.scalar_tensor_tensor(out=brow[:, 3, :], in0=brow[:, 3, :], scalar=0.5, in1=rows_in[:, 5, :],
                                   op0=ALU.mult, op1=ALU.add).then_inc(s_brow, 1)
            dve.wait_ge(s_bc, 1)
            V.tensor_copy(bc[:, :, :].rearrange("p k d -> p (k d)"), OP[0][0:P, :]).then_inc(s_bcs, 1)
            dve.wait_ge(s_win, 16 * G)
            for g in range(G):
                chain(V.scalar_tensor_tensor(out=win[:, g * CAP:(g + 1) * CAP],
                                             in0=window[:, g:g + 1].broadcast_to([P, CAP]), scalar=-float(WSPAN),
                                             in1=win[:, g * CAP:(g + 1) * CAP], op0=ALU.mult, op1=ALU.add))
            floor_div(win, q_f, rem_f, q_i, neg_f)
            chain(V.tensor_scalar(neg_f, q_f, 0.0, 0.0, ALU.is_ge, ALU.add, accum_out=c2[:, 0:1]))
            chain(V.tensor_scalar(neg_f, q_f, float(P), 0.0, ALU.is_ge, ALU.add, accum_out=c2[:, 1:2]))
            V.tensor_tensor(okc, c2[:, 0:1], c2[:, 1:2], ALU.subtract).then_inc(s_wkeys, 1)
            for n, (g, h) in enumerate([(g, h) for g in range(G) for h in range(HALVES)]):
                dve.wait_ge(s_wkt, n + 1)
                for v, keys in enumerate((row_key, col_key)):
                    V.tensor_copy(keys[:, h, g * P:(g + 1) * P], bank[n % 2][:, v * 128:v * 128 + P]).then_inc(s_wks, 1)
            dve.wait_ge(s_vtot, 1)
            chain(V.tensor_copy(total[:, :], OP[1][0:1, 0:1]))
            V.tensor_scalar(flag[:, :], total[:, :], float(E), None, ALU.is_equal).then_inc(s_flag, 1)
            V.memset(sums_out[:, :], 0.0).then_inc(s_acc, 1)
            dve.wait_ge(s_flag, 1)
            dve.wait_ge(s_wks, 2 * G * HALVES)
            dve.wait_ge(s_acc, 1)
            V.memset(tick[:, 5:6], 0.0).then_inc(s_ghot, 1)
            V.memset(tick[:, 6:7], 0.0).then_inc(s_ghotused, 1)
            fast = dve.value_load(flag[0:1, 0:1], min_val=0, max_val=1)

            def hot_keys(keys, first, n):
                return keys[:, :, bass.ds(first, n)].rearrange("p h w -> p w h")

            def step(k, b, t):
                for g in range(NG):
                    if has(t):
                        n = NG * t + g
                        q = (b + g) % 2
                        first = GW * n
                        with dve.If(fast):
                            ge(dve, s_built, n - 1)
                            for keys, hot in ((row_key, row_hot), (col_key, col_hot)):
                                kk = keys[:, :, cols(n, GW)].rearrange("p h w -> p w h")
                                ins = V.tensor_tensor(
                                    hot[:, q, :, :, :],
                                    iota_b[:, :].rearrange("p (a b k) -> p a b k", a=1, b=1).broadcast_to([128, GW, HALVES, P]),
                                    kk.rearrange("p w (h a) -> p w h a", a=1).broadcast_to([128, GW, HALVES, P]), ALU.is_equal)
                            ins.then_inc(s_hot, 1)
                        with dve.Else():
                            with dve.Fori(0, GW) as w:
                                ge(dve, s_ghot, (n * GW + w) * NB + 1)
                                V.tensor_scalar(gen_key, all_row[:, :], win_off[:, bass.ds(n * GW + w, 1)], None,
                                                ALU.subtract).then_inc(s_gkey, 1)
                                ge(dve, s_gkey, n * GW + w + 1)
                                carry(0)
                                with dve.Fori(0, NB) as c:
                                    ge(dve, s_ghotused, (n * GW + w) * NB + c + 1)
                                    io = iota_f[0:P, :].rearrange("p (a k) -> p a k", a=1).broadcast_to([P, GB, P])
                                    V.tensor_tensor(gen_row, io, gen_key[:, bass.ds(c * GB, GB)].rearrange(
                                        "p (c a) -> p c a", a=1).broadcast_to([P, GB, P]), ALU.is_equal)
                                    V.tensor_tensor(gen_col, io, all_col[:, bass.ds(c * GB, GB)].rearrange(
                                        "p (c a) -> p c a", a=1).broadcast_to([P, GB, P]), ALU.is_equal).then_inc(s_ghot, 1)
                    if has(t - 2):
                        for c in CHUNK_AT[g]:
                            m = NC * (t - 2) + c
                            c0, w = CHUNKS[c]
                            ge(dve, s_acc, m)
                            ge(dve, s_out, m + 1)
                            V.tensor_tensor(sums_out[:, c0:c0 + w], sums_out[:, c0:c0 + w], OP[(NC * b + c) % 2][:, 0:w],
                                            ALU.add).then_inc(s_acc, 1)
            steps(dve, step, T + 1)

            tail = Chain(dve, s_chain, chain.n)
            dve.wait_ge(s_ar, NG * T)
            dve.wait_ge(s_deg, T)
            dve.wait_ge(s_acc, NC * T + 1)
            tail(V.tensor_reduce(out=deg_in[:, :], in_=deg_part[:, :].rearrange("p (t g) -> p t g", g=NG), axis=AX, op=ALU.add))
            tail(V.tensor_reduce(out=deg_out[:, :], in_=deg_sum, axis=AX, op=ALU.add))
            for d in (deg_in, deg_out):
                tail(V.tensor_scalar(d[:, :], d[:, :], 1.0, None, ALU.max))
                tail(V.reciprocal(d[:, :], d[:, :]))

            def over_rows(v):
                return v.rearrange("p (k a) -> p k a", a=1).broadcast_to([P, 5, D])

            def over_tiles(i):
                return bc[:, i:i + 1, :].broadcast_to([P, 5, D])

            V.memset(tick[:, 6:7], 0.0).then_inc(s_tdone, 1)
            with dve.Fori(0, T // 5) as j:
                five = bass.ds(5 * j, 5)
                c5 = Chain(dve, s_tail, j * TAIL_STEPS)
                dve.wait_ge(s_tdone, j + 1)
                V.tensor_copy(so5[:, :, :].rearrange("p a b -> p (a b)"), sums_out[:, bass.ds(5 * P * j, 5 * P)]
                              ).then_inc(s_so5, 1)
                dve.wait_ge(s_x5, j + 1)
                dve.wait_ge(s_o5, j + 1)
                c5(V.tensor_tensor(y5[:, :, :], x5[:, :, :], slots(bank[2], P, w=D), ALU.add))
                for d, o in ((deg_in, bank[0]), (deg_out, bank[1])):
                    c5(V.tensor_tensor(t5[:, :, :], slots(o, P, w=D), over_rows(d[:, five]), ALU.mult))
                    c5(V.tensor_tensor(y5[:, :, :], y5[:, :, :], t5[:, :, :], ALU.add))
                c5(V.tensor_tensor(y5[:, :, :], y5[:, :, :], over_tiles(3), ALU.add))
                for i in range(5):
                    c5.add(V.bn_stats(st6[:, i, :], y5[:, i, :]))
                c5.wait()
                carry(1)
                for i in range(5):
                    c5.add(V.bn_aggr(mv[:, i, :], st6[:, i, :]))
                c5.wait()
                V.tensor_scalar(ve5[:, :], mv[:, :, 1], EPS, None, ALU.add).then_inc(s_ve5, 1)
                dve.wait_ge(s_rs5, j + 1)
                for i in range(5):
                    c5.add(V.tensor_scalar(y5[:, i, :], y5[:, i, :], mv[:, i, 0:1], rstd[:, i:i + 1],
                                           ALU.subtract, ALU.mult))
                c5.wait()
                V.tensor_copy(X1[:, five, :], y5[:, :, :]).then_inc(s_y5, 1)
                dve.wait_ge(s_h5s, j + 1)
                for i, a in ((0, a_s), (1, a_d)):
                    c5(V.tensor_tensor(t5[:, :, :], slots(bank[0], P, w=D), over_tiles(i), ALU.mult))
                    c5(V.tensor_reduce(out=a[:, five], in_=t5[:, :, :], axis=AX, op=ALU.add))
                assert c5.n == TAIL_STEPS
                V.memset(tick[:, 7:8], 0.0).then_inc(s_tdone, 1)

            for n, (c0, w) in enumerate(CHUNKS):
                h0, hn = c0 // P, w // P
                if n >= 2:
                    dve.wait_ge(s_arow, n - 1)
                V.tensor_tensor(diag[n % 2][0:P, 0:hn, :],
                                ident[0:P, 0:P].rearrange("p (a k) -> p a k", a=1).broadcast_to([P, hn, P]),
                                a_s[:, h0:h0 + hn].rearrange("p (k a) -> p k a", a=1).broadcast_to([P, hn, P]),
                                ALU.mult).then_inc(s_diag, 1)
                dve.wait_ge(s_arow, n + 1)
                V.tensor_copy(a_row[0:P, c0:c0 + w], OP[n % 2][0:P, 0:w]).then_inc(s_arows, 1)
            dve.wait_ge(s_arows, NC)

            LS = 5
            FS = 6

            def self_loops(k, b, t):
                n = k + 1
                dve.wait_ge(s_load[b], 16 * n)
                V.tensor_tensor(AR[b][:, cols(t, P)], AR[b][:, cols(t, P)], ident[0:P, 0:P], ALU.add
                                ).then_inc(s_self, 1)

            def maxima(t, b):
                c = Chain(dve, s_c2, t * LS)
                dve.wait_ge(s_pen, t + 1)
                carry(2 + b)
                c(V.tensor_tensor_reduce(out=S[b][:, :], in0=S[b][:, :], in1=a_row[0:P, :], scale=1.0, scalar=NEG,
                                         op0=ALU.add, op1=ALU.max, accum_out=mx[b][:, 0:1]))
                c(V.tensor_copy(mx[b][:, 3:4], a_d[:, cols(t, 1)]))
                c(V.tensor_tensor(mx[b][:, 1:2], mx[b][:, 0:1], mx[b][:, 3:4], ALU.add))
                c(V.tensor_scalar(mx[b][:, 2:3], mx[b][:, 1:2], -SLOPE, None, ALU.mult))
                c(V.scalar_tensor_tensor(out=mx[b][:, 2:3], in0=mx[b][:, 1:2], scalar=-1.0, in1=mx[b][:, 2:3],
                                         op0=ALU.mult, op1=ALU.min))
                V.scalar_tensor_tensor(out=mx[b][:, 2:3], in0=mx[b][:, 3:4], scalar=SLOPE, in1=mx[b][:, 2:3],
                                       op0=ALU.mult, op1=ALU.add).then_inc(s_m, 1)

            def leaky(t, b):
                dve.wait_ge(s_relu, t + 1)
                V.scalar_tensor_tensor(out=S[b][:, :], in0=S[b][:, :], scalar=SLOPE / (1.0 - SLOPE), in1=R[b],
                                       op0=ALU.mult, op1=ALU.add).then_inc(s_lr, 1)

            def weights(t, b):
                dve.wait_ge(s_e, t + 1)
                V.tensor_tensor(S[b][:, :], S[b][:, :], AR[b][:, :], ALU.mult).then_inc(s_p, 1)

            def evict(t, b, g):
                dve.wait_ge(s_t2, NG * t + g + 1)
                ge(dve, s_mm, NG * t + g - 1)
                q = (b + g) % 2
                V.tensor_copy(PT[q][:, :, :], slots(bank[q], P)).then_inc(s_evd, 1)

            def finish(k, b, t):
                c = Chain(dve, s_f2, t * FS)
                o = OP[b]
                dve.wait_ge(s_mm, NG * (t + 1))
                ge(dve, s_res[b], 16 * k)
                c(V.tensor_scalar(rden[b][:, :], o[0:P, D:D + 1], 1e-16, None, ALU.add))
                c(V.reciprocal(rden[b][:, :], rden[b][:, :]))
                c(V.scalar_tensor_tensor(out=fin[b][:, :], in0=o[0:P, 0:D], scalar=rden[b][:, 0:1], in1=bc[:, 2, :],
                                         op0=ALU.mult, op1=ALU.add))
                c(V.tensor_tensor(fin[b][:, :], fin[b][:, :], X1[:, (t if isinstance(t, int) else bass.ds(t, 1)), :]
                                  if isinstance(t, int) else X1[:, bass.ds(t, 1), :].rearrange("p a d -> p (a d)"), ALU.add))
                c(V.bn_stats(st2[b][:, :], fin[b][:, :]))
                carry(4 + b)
                c(V.bn_aggr(mv2[b][:, :], st2[b][:, :]))
                V.tensor_scalar(ve2[b][:, :], mv2[b][:, 1:2], EPS, None, ALU.add).then_inc(s_ve2, 1)

            def normalize(t, b):
                dve.wait_ge(s_rs2, t + 1)
                V.tensor_scalar(fin[b][:, :], fin[b][:, :], mv2[b][:, 0:1], rs2[b][:, 0:1],
                                ALU.subtract, ALU.mult).then_inc(s_fin, 1)

            self_loops(0, 0, 0)
            self_loops(0, 1, 1)
            maxima(0, 0)
            leaky(0, 0)
            weights(0, 0)

            def step2(k, b, t):
                if has(t - 2):
                    normalize(t - 2, b)
                if has(t + 1):
                    maxima(t + 1, 1 - b)
                if has(t):
                    evict(t, b, 2)
                if has(t + 1):
                    leaky(t + 1, 1 - b)
                if has(t):
                    evict(t, b, 3)
                if has(t - 1):
                    finish(k - 1 + b, 1 - b, t - 1)
                if has(t + 1):
                    weights(t + 1, 1 - b)
                if has(t + 2):
                    self_loops(k + 1, b, t + 2)
            steps(dve, step2, T + 1)

        @block.tensor
        def _(pe):
            M = nc.tensor
            pe.wait_ge(s_hb0, 1)
            M.matmul(AI[0:P, 0:P], ones[:, :], heads, start=True, stop=True).then_inc(s_hb, 1)
            pe.wait_ge(s_ld["w"], 64)
            pe.wait_ge(s_rowno, 1)
            for k in range(3):
                ins = M.transpose(AI[:, k * D:(k + 1) * D], Wst[k][:, :], ident[:, :])
            ins.then_inc(s_wt, 1)
            pe.wait_ge(s_brow, 1)
            M.matmul(OP[0][0:P, :], ones_row[:, :], brow[:, :, :].rearrange("p k d -> p (k d)"), start=True, stop=True
                     ).then_inc(s_bc, 1)
            pe.wait_ge(s_wkeys, 1)
            for n, (g, h) in enumerate([(g, h) for g in range(G) for h in range(HALVES)]):
                if n >= 2:
                    pe.wait_ge(s_wks, 2 * (n - 1))
                for v, keys in enumerate((q_f, rem_f)):
                    ins = M.transpose(bank[n % 2][:, v * 128:v * 128 + P],
                                      keys[:, g * CAP + h * 128:g * CAP + (h + 1) * 128], ident[0:P, 0:P])
                ins.then_inc(s_wkt, 1)
            M.matmul(OP[1][0:1, 0:1], okc, ones[:, 0:1], start=True, stop=True).then_inc(s_vtot, 1)
            pe.wait_ge(s_wks, 2 * G * HALVES)
            pe.wait_ge(s_wts, 3)
            pe.wait_ge(s_bcs, 1)
            pe.wait_ge(s_ld["x"], 16)
            pe.wait_ge(s_flag, 1)
            fast = pe.value_load(flag[0:1, 0:1], min_val=0, max_val=1)

            def step(k, b, t):
                for g in range(NG):
                    if has(t):
                        n = NG * t + g
                        q = (b + g) % 2
                        ge(pe, s_at, n)
                        with pe.If(fast):
                            ge(pe, s_hot, n + 1)
                            for w in range(GW):
                                for h in range(HALVES):
                                    ins = M.matmul(BP[0:P, w * 128:w * 128 + P], col_hot[:, q, w, h, :], row_hot[:, q, w, h, :],
                                                   start=(h == 0), stop=(h == HALVES - 1))
                            ins.then_inc(s_built, 1)
                        with pe.Else():
                            with pe.Fori(0, GW) as w:
                                o = BP[0:P, bass.ds(w * 128, P)]
                                M.matmul(o, zero_w[:, :], zero_w[:, :], start=True, stop=False)
                                with pe.Fori(0, NB) as c:
                                    ge(pe, s_ghot, (n * GW + w) * NB + c + 2)
                                    for e in range(GB):
                                        ins = M.matmul(o, gen_col[:, e, :], gen_row[:, e, :], start=False, stop=False)
                                    ins.then_inc(s_ghotused, 1)
                                M.matmul(o, zero_w[:, :], zero_w[:, :], start=False, stop=True)
                            M.matmul(OPX, zero_w[:, 0:1], zero_w[:, 0:1], start=True, stop=True).then_inc(s_built, 1)
                    if has(t - 1):
                        u = NG * (t - 1) + g
                        a = AT[1 - b]
                        ge(pe, s_at, NG * t)
                        ge(pe, s_ar, u)
                        for i in range(5):
                            ins = M.transpose(TP[0:P, i * 128:i * 128 + P], a[:, 5 * g + i, :], ident[0:P, 0:P])
                        ins.then_inc(s_tp, 1)
                        if g == 0:
                            ge(pe, s_agin, t - 1)
                        for i in range(5):
                            h = 5 * g + i
                            ins = M.matmul(AI[:, 0:P], X[:, h, :], a[:, h, :], start=(h == 0), stop=(h == T - 1))
                        if g == NG - 1:
                            ins.then_inc(s_ai, 1)
                    if has(t - 2):
                        if g == 0:
                            ge(pe, s_ar, NG * (t - 1))
                            pe.wait_ge(s_xt[b], 16 * k)
                        for c in CHUNK_AT[g]:
                            c0, w = CHUNKS[c]
                            ge(pe, s_acc, NC * (t - 2) + c)
                            M.matmul(OP[(NC * b + c) % 2][:, 0:w], xt[b][:, :], AR[b][:, c0:c0 + w],
                                     start=True, stop=True).then_inc(s_out, 1)
            steps(pe, step, T + 1)

            pe.wait_ge(s_acc, NC * T + 1)
            pe.wait_ge(s_agin, T)
            with pe.Fori(0, T // 5) as j:
                pe.wait_ge(s_x5, j + 1)
                for i in range(5):
                    ins = M.transpose(bank[3][:, i * 128:i * 128 + P], x5[:, i, :], ident[0:P, 0:P])
                ins.then_inc(s_x5T, 1)
                pe.wait_ge(s_si5, j + 1)
                for i in range(5):
                    M.matmul(bank[0][0:P, i * 128:(i + 1) * 128], si5[:, i, :], WiT[:, :], start=True, stop=True)
                pe.wait_ge(s_so5, j + 1)
                for i in range(5):
                    M.matmul(bank[1][0:P, i * 128:(i + 1) * 128], so5[:, i, :], WoT[:, :], start=True, stop=True)
                pe.wait_ge(s_x5Ts, j + 1)
                for i in range(5):
                    ins = M.matmul(bank[2][0:P, i * 128:(i + 1) * 128], x5T[:, i, :], WrT[:, :], start=True, stop=True)
                ins.then_inc(s_o5, 1)
                pe.wait_ge(s_y5, j + 1)
                for i in range(5):
                    ins = M.transpose(bank[3][:, i * 128:i * 128 + P], y5[:, i, :], ident[0:P, 0:P])
                ins.then_inc(s_y5T, 1)
                pe.wait_ge(s_y5Ts, j + 1)
                for i in range(5):
                    ins = M.matmul(bank[0][0:P, i * 128:(i + 1) * 128], x5T[:, i, :], Wg[:, :], start=True, stop=True)
                ins.then_inc(s_h5, 1)

            for n, (c0, w) in enumerate(CHUNKS):
                pe.wait_ge(s_diag, n + 1)
                if n >= 2:
                    pe.wait_ge(s_arows, n - 1)
                M.matmul(OP[n % 2][0:P, 0:w], ones[:, :], diag[n % 2][0:P, 0:w // P, :].rearrange("p k j -> p (k j)"),
                         start=True, stop=True).then_inc(s_arow, 1)
            pe.wait_ge(s_arows, NC)

            def transposes(t, b, g):
                q = (b + g) % 2
                if g == 0:
                    pe.wait_ge(s_p, t + 1)
                if g == 2 or g == 3:
                    pe.wait_ge(s_eva, 3 * t + g - 1)
                elif g == 4:
                    pe.wait_ge(s_evd, 2 * t + 1)
                elif g == 0:
                    ge(pe, s_evd, 2 * t)
                else:
                    ge(pe, s_eva, 3 * t)
                for i in range(5):
                    h = 5 * g + i
                    ins = M.transpose(bank[q][0:P, i * 128:i * 128 + P], S[b][:, h * P:(h + 1) * P], ident[0:P, 0:P])
                ins.then_inc(s_t2, 1)

            transposes(0, 0, 0)

            def step2(k, b, t):
                for g in range(NG):
                    if g < NG - 1:
                        transposes(t, b, g + 1)
                    elif has(t + 1):
                        transposes(t + 1, 1 - b, 0)
                    if g == 0:
                        ge(pe, s_ve2, t - 1)
                    if g in (2, 3):
                        pe.wait_ge(s_evd, 2 * t + g - 1)
                    else:
                        pe.wait_ge(s_eva, 3 * t + (3 if g == 4 else g + 1))
                    for i in range(5):
                        h = 5 * g + i
                        ins = M.matmul(OP[b][0:P, 0:D + 1], PT[(b + g) % 2][:, i, :], H[:, h, :],
                                       start=(h == 0), stop=(h == T - 1))
                    ins.then_inc(s_mm, 1)
            steps(pe, step2, T - 1)


_INS = ["x", "src", "dst", "L0_gnn_W_in", "L0_gnn_b_in", "L0_gnn_W_out", "L0_gnn_b_out", "L0_gnn_W_root",
        "L0_gnn_b_root", "L1_gnn_W", "L1_gnn_att_src", "L1_gnn_att_dst", "L1_gnn_bias"]


def kernel(**inputs):
    import numpy as _np
    import concourse.bacc as _bacc
    from concourse import mybir as _mybir
    from concourse.bass_utils import run_bass_kernel_spmd as _run

    nc = _bacc.Bacc("TRN2", target_bir_lowering=False, num_devices=1)
    arrays, args = {}, []
    for name in _INS:
        a = _np.ascontiguousarray(inputs[name])
        arrays[f"in_{name}_dram"] = a
        args.append(nc.dram_tensor(f"in_{name}_dram", a.shape, _mybir.dt.from_np(a.dtype), kind="ExternalInput").ap())
    args.append(nc.dram_tensor("out_dram", tuple(inputs["x"].shape), _mybir.dt.float32, kind="ExternalOutput").ap())
    x, src, dst, W_in, b_in, W_out, b_out, W_root, b_root, W_gat, att_src, att_dst, b_gat, out = args
    gnn_resnorm_kernel(nc, x, src, dst, W_in, b_in, W_out, b_out, W_root, b_root, W_gat, att_src, att_dst,
                       b_gat, out)
    r = _run(nc, [arrays], core_ids=[0])
    return r.results[0]["out_dram"]
```

```python
import concourse.bass as bass
from concourse import mybir
from contextlib import ExitStack


def gnn_resnorm_kernel(nc, x, src, dst, W_in, b_in, W_out, b_out, W_root, b_root,
                       W_gat, att_src, att_dst, b_gat, out):
    f32, bf16, i32 = mybir.dt.float32, mybir.dt.bfloat16, mybir.dt.int32
    ALU = mybir.AluOpType
    ACT = mybir.ActivationFunctionType
    AX = mybir.AxisListType.X

    N, D = x.shape
    E = src.shape[0]
    P = 125
    T = N // P
    EC = E // P
    WN = P // T
    NW = N // WN
    G = NW // P
    GW = P // WN // 5
    NG = 5
    CAP = 256
    HALVES = 2
    ALIGN = 32
    NR = E // ALIGN + 1
    PAD = (NR - 1) * ALIGN + CAP - E
    WSPAN = WN * N
    CH = 500
    CHUNKS = [(c, min(CH, N - c)) for c in range(0, N, CH)]
    NC = len(CHUNKS)
    CHUNK_AT = [[0, 1], [2, 3], [4], [5], [6]]
    GB = 15
    NB = EC // GB
    NEG = -1.0e30
    SLOPE = 0.2
    EPS = 1e-5
    CONSTS = 11
    assert T * P == N and P * EC == E and WN * T == P and NB * GB == EC

    flat_keys = nc.dram_tensor("flat_keys", [E + PAD], f32, kind="Internal").ap()
    key_rows = nc.dram_tensor("key_rows", [NR, CAP], f32, kind="Internal").ap()
    counts = nc.dram_tensor("counts", [N, N], f32, kind="Internal").ap()
    counts_b = nc.dram_tensor("counts_b", [N, N], bf16, kind="Internal").ap()

    ctx = ExitStack()
    with ctx:
        def sb(name, shape, dt=f32):
            return ctx.enter_context(nc.sbuf_tensor(name, shape, dt))

        def sem(name):
            return ctx.enter_context(nc.semaphore(name))

        X = sb("X", [P, T, D])
        X1f = sb("X1", [P, T * D])
        X1 = X1f[:, :].rearrange("p (t d) -> p t d", t=T)
        H = sb("H", [P, T, D + 1])
        sums_in = sb("sums_in", [D, N])
        sums_out = sb("sums_out", [D, N])
        AT = [sb(f"AT{b}", [P, T, P]) for b in range(2)]
        NA = -(-N // 64) * 64
        AR_all = [sb(f"AR{b}", [P, NA]) for b in range(2)]
        AR = [a[:, 0:N] for a in AR_all]
        S = [sb(f"S{b}", [P, N]) for b in range(2)]
        xt = [sb(f"xt{b}", [P, D]) for b in range(2)]
        KEYS, HOTS = NW * HALVES, 2 * GW * 128 * HALVES
        window_space = sb("window_space", [128, 2 * KEYS + 2 * HOTS], bf16)
        row_key, col_key = [window_space[:, i * KEYS:(i + 1) * KEYS].rearrange("p (w h) -> p w h", h=HALVES)
                            for i in range(2)]
        row_hot, col_hot = [window_space[:, 2 * KEYS + i * HOTS:2 * KEYS + (i + 1) * HOTS]
                            .rearrange("p (q w k h) -> p q w k h", q=2, w=GW, k=128) for i in range(2)]
        all_row = sb("all_row", [P, EC])
        all_col = sb("all_col", [P, EC])
        iota_b = sb("iota_b", [128, 128, HALVES], bf16)
        iota_f = sb("iota_f", [128, 128])
        iota_i = sb("iota_i", [128, 128], i32)
        window_i = sb("window_i", [P, G], i32)
        window = sb("window", [P, G])
        ident = sb("ident", [128, 128])
        ones = sb("ones", [P, P])
        ones_row = sb("ones_row", [1, 128])
        WiT = sb("WiT", [D, D])
        WoT = sb("WoT", [D, D])
        WrT = sb("WrT", [D, D])
        Wg = sb("Wg", [D, D])
        rows_in = sb("rows_in", [1, 6, D])
        brow = sb("brow", [1, 4, D])
        bc = sb("bc", [P, 4, D])
        x5T = sb("x5T", [D, 5, P])
        parts = sb("parts", [P, T * 3 * D // 2])
        X3 = parts[:, :].bitcast(bf16).rearrange("p (t i d) -> p t i d", t=T, i=3)
        PT = [parts[:, g * 5 * P:(g + 1) * 5 * P].rearrange("p (k j) -> p k j", k=5)
              for g in range(NG)]
        X3f = parts[:, :].bitcast(bf16)
        xt3 = [sb(f"xt3{b}", [P, 3, D], bf16) for b in range(2)]
        ident_b = sb("ident_b", [P, P], bf16)
        deg_part = sb("deg_part", [P, T * NG])
        deg_in = sb("deg_in", [P, T])
        deg_out = sb("deg_out", [P, T])
        a_d = sb("a_d", [P, T])
        slope_ad = sb("slope_ad", [P, T])
        relu_ad = sb("relu_ad", [P, T])
        Wa = sb("Wa", [D, 2])
        Wa_wide = sb("Wa_wide", [D, P])
        Wx = sb("Wx", [D, D])
        bcD = sb("bcD", [D, 2, D])
        st6 = sb("st6", [P, 5, 6])
        mv = sb("mv", [P, 5, 2])
        rstd = sb("rstd", [P, 5])
        ve5 = sb("ve5", [P, 5])
        mhalf = sb("mhalf", [P, 5])
        mx = [sb(f"mx{b}", [P, 4]) for b in range(2)]
        fin = [sb(f"fin{b}", [P, D]) for b in range(2)]
        rden = [sb(f"rden{b}", [P, 1]) for b in range(2)]
        st2 = [sb(f"st2{b}", [P, 6]) for b in range(2)]
        mv2 = [sb(f"mv2{b}", [P, 2]) for b in range(2)]
        ve2 = [sb(f"ve2{b}", [P, 1]) for b in range(2)]
        rs2 = [sb(f"rs2{b}", [P, 1]) for b in range(2)]
        total = sb("total", [1, 1])
        tick = sb("tick", [1, 8])
        flag = sb("flag", [1, 1], i32)
        R = [sums_in[0:P, :], X[:, :, :].rearrange("p t d -> p (t d)")[:, 0:N]]
        AT_b = [AT[b][:, :, :].rearrange("p a b -> p (a b)").bitcast(bf16)[:, 0:T * P]
                .rearrange("p (a b) -> p a b", a=T) for b in range(2)]
        AR_b = [AR_all[i // 2][:, :].bitcast(bf16)[:, i % 2 * NA:i % 2 * NA + N] for i in range(4)]
        pen = [window_space[0:P, b * N:(b + 1) * N] for b in range(2)]
        V2 = [AT[b][:, :, :].rearrange("p a b -> p (a b)") for b in range(2)]
        deg_sum = X1[:, :, 0:P]
        a_row = sums_out
        dst_i = S[0][:, 0:EC].bitcast(i32)
        src_i = S[0][:, EC:2 * EC].bitcast(i32)
        flat = S[0][:, 2 * EC:3 * EC]
        q_i = AR[1][:, 0:G * CAP].bitcast(i32)
        q_f = AR[1][:, G * CAP:2 * G * CAP]
        neg_f = AT[0][:, :, :].rearrange("p a b -> p (a b)")[:, 0:G * CAP]
        rem_f = AT[1][:, :, :].rearrange("p a b -> p (a b)")[:, 0:G * CAP]
        win = AT[1][:, :, :].rearrange("p a b -> p (a b)")[:, G * CAP:2 * G * CAP]
        cand = [b[:, k * EC:(k + 1) * EC].bitcast(i32) for b, k in ((S[1], 0), (S[1], 1), (S[1], 2), (sums_in[0:P, :], 0),
                                                                     (sums_in[0:P, :], 1))]
        cmp_f = sums_out[0:P, 0:EC]
        all_src = S[1][:, 0:EC]
        heads = AR[0][:, 128:128 + P]
        pad = sums_out[0:1, EC:EC + PAD]
        wbase = AR[0][:, 0:G]
        krow = AR[0][:, 8:8 + G]
        rowno = AR[0][:, 16:16 + G]
        start = AR[0][:, 24:24 + G]
        rowno_i = AR[0][:, 32:32 + G].bitcast(i32)
        start_i = AR[0][:, 40:40 + G].bitcast(i32)
        c2 = AR[0][:, 48:48 + G]
        okc = AR[0][:, 56:57]
        Wst = [sb(f"Wst{k}", [D, D]) for k in range(3)]
        gen_row = S[0][:, 0:GB * P].rearrange("p (c k) -> p c k", c=GB)
        gen_col = S[1][:, 0:GB * P].rearrange("p (c k) -> p c k", c=GB)
        gen_key = S[0][:, GB * P:GB * P + EC]
        zero_w = sb("zero_w", [P, P])
        win_off = sb("win_off", [P, NW])
        win_off_i = S[1][:, 3 * EC:3 * EC + NW].bitcast(i32)

        bank = [ctx.enter_context(nc.psum_tensor(f"bank{k}", [128, 1024], f32)) for k in range(4)]
        BP, TP = bank[0], bank[1]
        OP = [bank[2][:, 0:512], bank[2][:, 512:1024]]
        AI = bank[3][:, 0:512]
        OPX = bank[3][0:1, 512:513]

        TSLOT = [bank[0], bank[1], bank[3], bank[0], bank[1]]
        HALF = 625
        LC = 1625

        def slots_b(b):
            return b[0:P, 0:320].bitcast(bf16).rearrange("p (k j) -> p k j", j=128)[:, :, 0:P]

        def slots(b, rows, n=5, w=P):
            return b[0:rows, 0:n * 128].rearrange("p (k j) -> p k j", j=128)[:, :, 0:w]

        s_ld = {k: sem("loaded_" + k) for k in ("dst", "src", "w", "rows", "x")}
        s_xt = [sem("xt_loaded0"), sem("xt_loaded1")]
        s_const = sem("constants_made")
        s_chain = sem("prelude_vector_step")
        s_hb0 = sem("heads_converted")
        s_brow = sem("constant_rows_made")
        s_bc = sem("constant_rows_spread")
        s_bcs = sem("constant_rows_saved")
        s_f2 = sem("layer2_finish_step")
        s_wt = sem("weights_transposed_L1")
        s_wts = sem("weights_saved")
        s_hb = sem("heads_on_every_row")
        s_wre = sem("identity_in_W_root")
        s_hbias = sem("bias_added_to_H")
        s_gdec = sem("general_keys_step")
        s_flatk = sem("flat_keys_made")
        s_flat = sem("flat_keys_stored")
        s_rows = sem("key_rows_stored")
        s_rowno = sem("candidate_rows_known")
        s_cand = [sem(f"candidate_rows_loaded{g}") for g in range(G)]
        s_start = sem("window_starts_known")
        s_win = sem("windows_loaded")
        s_wkeys = sem("window_keys_made")
        s_wkt = sem("window_keys_transposed")
        s_wks = sem("window_keys_saved")
        s_vsum = sem("valid_edges_counted")
        s_vtot = sem("valid_edges_summed")
        s_flag = sem("flag_known")
        s_hot = sem("onehots_ready")
        s_gkey = sem("general_keys_ready")
        s_ghot = sem("general_onehots_ready")
        s_ghotused = sem("general_onehots_used")
        s_built = sem("window_counts_built")
        s_at = sem("AT_group_ready")
        s_tp = sem("AR_group_transposed")
        s_ar = sem("AR_group_ready")
        s_ai = sem("sums_in_tile_done")
        s_agin = sem("sums_in_tile_saved")
        s_out = sem("sums_out_chunk_done")
        s_acc = sem("sums_out_chunk_added")
        s_deg = sem("degree_added")
        s_degz = sem("degree_zeroed")
        s_store = [sem("counts_stored0"), sem("counts_stored1")]
        s_root = sem("x_W_root_saved")
        s_mean5 = sem("tail_means_projected")
        s_sum5 = sem("tail_summed")
        s_x5T = sem("tail_xT_transposed")
        s_x5Ts = sem("tail_xT_saved")
        s_o5 = sem("tail_products_done")
        s_ve5 = sem("tail_variance")
        s_rs5 = sem("tail_rstd")
        s_y5 = sem("tail_normalized")
        s_x1b = sem("bias_added_to_x1")
        s_y5T = sem("tail_yT_transposed")
        s_y5Ts = sem("tail_yT_saved")
        s_h5 = sem("tail_h_done")
        s_h5s = sem("tail_h_saved")
        s_arow = sem("a_s_row_done")
        s_arows = sem("a_s_row_saved")
        s_load = [sem(f"counts_loaded{i}") for i in range(4)]
        s_parts = sem("x_parts_step")
        s_x3 = sem("x_parts_of_tile_ready")
        s_self = sem("self_loops_added_for_mask")
        s_wself = sem("self_loops_added_for_weights")
        s_pen = sem("mask_ready")
        s_m = sem("max_ready")
        s_bias = sem("exp_bias_ready")
        s_relu = sem("relu_of_first_columns_done")
        s_relup = sem("relu_of_last_columns_done")
        s_lr = sem("leaky_first_columns_done")
        s_lrp = sem("leaky_last_columns_done")
        s_e = sem("exp_done")
        s_p = sem("weights_ready_first_groups")
        s_pp = sem("weights_ready_last_groups")
        s_t2 = sem("weights_transposed")
        s_ev = sem("transposed_weights_saved")
        s_mm = sem("PT_used")
        s_c2 = sem("layer2_vector_step")
        s_ve2 = sem("layer2_variance")
        s_rs2 = sem("layer2_rstd")
        s_fin = sem("row_tile_ready")
        s_res = [sem("result_stored0"), sem("result_stored1")]

        def ge(eng, s, v):
            if not isinstance(v, int) or v > 0:
                eng.wait_ge(s, v)

        def carry(i):
            nc.vector.memset(tick[:, i:i + 1], 0.0)

        class Chain:
            def __init__(self, eng, s, base=0):
                self.eng, self.s, self.base, self.n = eng, s, base, 0

            def add(self, ins):
                ins.then_inc(self.s, 1)
                self.n += 1

            def wait(self):
                self.eng.wait_ge(self.s, self.base + self.n)

            def __call__(self, ins):
                self.add(ins)
                self.wait()

        def steps(eng, body, last, period=2):
            end = 22 if period == 2 else 20
            for t in range(4):
                body(t // period, t % period, t)
            with eng.Fori(4 // period, end // period) as k:
                for b in range(period):
                    body(k, b, period * k + b)
            for t in range(end, last + 1):
                body(t // period, t % period, t)

        def nth(k, b, off, m):
            return (4 // m) * k + (b + off) // m

        def in_mode(eng, body):
            fast = eng.value_load(flag[0:1, 0:1], min_val=0, max_val=1)
            with eng.If(fast):
                body(True)
            with eng.Else():
                body(False)

        def has(t, lo=0):
            return not isinstance(t, int) or lo <= t < T

        def cols(t, w):
            return slice(t * w, (t + 1) * w) if isinstance(t, int) else bass.ds(t * w, w)

        block = ctx.enter_context(nc.Block())
        xv = x.rearrange("(t p) d -> p t d", p=P)

        @block.sync
        def _(sp):
            sp.dma_start(dst_i, dst.rearrange("(p c) -> p c", c=EC)).then_inc(s_ld["dst"], 16)
            sp.dma_start(src_i, src.rearrange("(p c) -> p c", c=EC)).then_inc(s_ld["src"], 16)
            sp.dma_start(X[:, :, :], xv).then_inc(s_ld["x"], 16)
            for k, w in enumerate((W_in, W_out, W_root)):
                sp.dma_start(Wst[k][:, :], w).then_inc(s_ld["w"], 16)
            sp.dma_start(Wg[:, :], W_gat).then_inc(s_ld["w"], 16)
            for k, r in enumerate((att_src, att_dst, b_gat, b_in, b_out, b_root)):
                sp.dma_start(rows_in[:, k, :], r.rearrange("(a d) -> a d", a=1)).then_inc(s_ld["rows"], 16)
            sp.wait_ge(s_flatk, 1)
            sp.dma_start(flat_keys[0:E].rearrange("(p c) -> p c", c=EC), flat).then_inc(s_flat, 16)
            sp.wait_ge(s_const, CONSTS)
            sp.dma_start(flat_keys[E:E + PAD].rearrange("(a c) -> a c", a=1), pad).then_inc(s_flat, 16)
            sp.wait_ge(s_cand[G - 2], 16)
            sp.wait_ge(s_flat, 32)
            overlapping = bass.AP(flat_keys.tensor, 0, [[ALIGN, NR], [1, CAP]])
            sp.dma_start(key_rows, overlapping).then_inc(s_rows, 16)

            sp.wait_ge(s_flag, 1)

            def main(fast):
                def step(k, b, t):
                    if has(t) and not fast:
                        ge(sp, s_out, NC * (t - 1))
                        sp.dma_start(xt[b][:, :], x[cols(t, P), :]).then_inc(s_xt[b], 16)
                    if has(t - 1):
                        ge(sp, s_ar, NG * t)
                        c, a = (counts_b, AR_b) if fast else (counts, AR)
                        sp.dma_start(c[cols(t - 1, P), :], a[1 - b][:, :]).then_inc(s_store[1 - b], 16)
                steps(sp, step, T)
                sp.wait_ge(s_store[0], 16 * 13)
                sp.wait_ge(s_store[1], 16 * 12)
                sp.wait_ge(s_out, NC * T)

                if fast:
                    for t in range(4):
                        sp.dma_start(AR_b[t][:, :], counts_b[cols(t, P), :]).then_inc(s_load[t], 16)
                else:
                    sp.dma_start(AR[1][:, :], counts[cols(0, P), :]).then_inc(s_load[1], 16)
                    for t in range(4):
                        ge(sp, s_pen, t)
                        sp.dma_start(AR[0][:, :], counts[cols(t, P), :]).then_inc(s_load[0], 16)

                def step2(k, b, t):
                    if has(t + 1):
                        sp.wait_ge(s_p, t + 1)
                        sp.wait_ge(s_pp, t + 1)
                    if fast and has(t + 4):
                        sp.dma_start(AR_b[b][:, :], counts_b[cols(t + 4, P), :]).then_inc(s_load[b], 16)
                    if not fast and has(t + 1):
                        sp.dma_start(AR[1][:, :], counts[cols(t + 1, P), :]).then_inc(s_load[1], 16)
                    if not fast and has(t + 4):
                        sp.wait_ge(s_pen, t + 4)
                        sp.dma_start(AR[0][:, :], counts[cols(t + 4, P), :]).then_inc(s_load[0], 16)
                    if has(t - 2):
                        ge(sp, s_fin, t - 1)
                        sp.dma_start(out[cols(t - 2, P), :], fin[b % 2][:, :]).then_inc(s_res[b % 2], 16)
                steps(sp, step2, T + 1, 4)
                sp.wait_ge(s_res[0], 16 * 13)
                sp.wait_ge(s_res[1], 16 * 12)

            in_mode(sp, main)

        @block.gpsimd
        def _(pool):
            pool.memset(ident[:, :], 0.0).then_inc(s_const, 1)
            pool.wait_ge(s_const, 1)
            pool.affine_select(out=ident[:, :], in_=ident[:, :], compare_op=ALU.not_equal, fill=1.0,
                               base=0, pattern=[[-1, 128]], channel_multiplier=1).then_inc(s_const, 1)
            pool.iota(iota_i[:, :], pattern=[[1, 128]], base=0, channel_multiplier=0).then_inc(s_const, 1)
            pool.iota(window_i[:, :], pattern=[[P, G]], base=0, channel_multiplier=1).then_inc(s_const, 1)
            pool.iota(win_off_i, pattern=[[P, NW]], base=0, channel_multiplier=0).then_inc(s_const, 1)
            for tile, v in ((ones[:, :], 1.0), (ones_row[:, :], 1.0), (pad, -1.0e6), (zero_w[:, :], 0.0),
                            (mhalf[:, :], -0.5), (H[:, :, D:D + 1], 1.0)):
                pool.memset(tile, v).then_inc(s_const, 1)
            pool.wait_ge(s_rowno, 1)
            for g in range(G):
                pool.indirect_dma_start(cand[g], None, dst.rearrange("(p c) -> p c", c=EC),
                                        bass.IndirectOffsetOnAxis(ap=rowno_i[:, g:g + 1], axis=0)
                                        ).then_inc(s_cand[g], 16)
            pool.wait_ge(s_start, 1)
            pool.wait_ge(s_rows, 16)
            for g in range(G):
                pool.indirect_dma_start(win[:, g * CAP:(g + 1) * CAP], None, key_rows,
                                        bass.IndirectOffsetOnAxis(ap=start_i[:, g:g + 1], axis=0)
                                        ).then_inc(s_win, 16)
            pool.wait_ge(s_parts, 3)
            pool.tensor_tensor(X3[:, :, 2, :], X1[:, :, :], X3[:, :, 1, :], ALU.subtract).then_inc(s_parts, 1)
            pool.wait_ge(s_parts, 4)
            pool.memset(deg_sum, 0.0).then_inc(s_degz, 1)
            pool.wait_ge(s_root, T // 5)
            pool.wait_ge(s_bcs, 1)
            pool.tensor_tensor(H[:, :, 0:D], H[:, :, 0:D], bc[:, 3:4, :].broadcast_to([P, T, D]), ALU.add).then_inc(s_hbias, 1)

            pool.wait_ge(s_flag, 1)
            pool.wait_ge(s_degz, 1)

            def main(fast):
                def step(k, b, t):
                    if not has(t - 1):
                        return
                    ge(pool, s_at, NG * t)
                    ge(pool, s_deg, t - 1)
                    a = AT_b if fast else AT
                    pool.tensor_tensor(deg_sum, deg_sum, a[1 - b][:, :, :], ALU.add).then_inc(s_deg, 1)
                steps(pool, step, T)

            in_mode(pool, main)

            for j in range(T // 5):
                pool.wait_ge(s_ve5, j + 1)
                pool.tensor_tensor(rstd[:, :], ve5[:, :], mhalf[:, 0:5], ALU.pow).then_inc(s_rs5, 1)
            pool.wait_ge(s_y5T, T // 5)
            pool.tensor_tensor(X1[:, :, :], X1[:, :, :], bc[:, 2:3, :].broadcast_to([P, T, D]), ALU.add).then_inc(s_x1b, 1)


            def layer2(fast):
                def weigh(t, b):
                    a = AR_b[b] if fast else AR[1]
                    v = V2[b % 2]
                    pool.wait_ge(s_e, t + 1)
                    if not fast:
                        pool.wait_ge(s_wself, t + 1)
                    pool.tensor_tensor(v[:, HALF:N], v[:, HALF:N], a[:, HALF:N], ALU.mult).then_inc(s_pp, 1)

                def leaky(t, b):
                    pool.wait_ge(s_relup, t + 1)
                    pool.tensor_tensor(R[b][:, LC:N], S[b][:, LC:N], R[b][:, LC:N], ALU.add).then_inc(s_lrp, 1)

                leaky(0, 0)
                leaky(1, 1)

                def step2(k, b, t):
                    if has(t - 3):
                        i = (b + 1) % 2
                        pool.wait_ge(s_ve2, t - 2)
                        pool.tensor_tensor(rs2[i][:, :], ve2[i][:, :], mhalf[:, 0:1], ALU.pow).then_inc(s_rs2, 1)
                    if has(t):
                        weigh(t, b)
                    if has(t + 2):
                        leaky(t + 2, b % 2)
                steps(pool, step2, T + 2, 4)

            in_mode(pool, layer2)

        @block.scalar
        def _(act):
            act.wait_ge(s_ld["x"], 16)
            act.activation(X3[:, :, 0, :], X[:, :, :], ACT.Copy).then_inc(s_parts, 1)
            act.wait_ge(s_wt, 1)
            for k, w, f in ((2, WrT, 1.0), (0, WiT, 0.5), (1, WoT, 0.5)):
                act.activation(w[:, :], AI[:, k * D:(k + 1) * D], ACT.Copy, scale=f).then_inc(s_wts, 1)
            for j in range(T // 5):
                act.wait_ge(s_x5T, j + 1)
                if j:
                    act.wait_ge(s_o5, j)
                act.activation(x5T[:, :, :], slots(bank[0], D), ACT.Copy).then_inc(s_x5Ts, 1)
                if j:
                    act.activation(H[:, 5 * j - 5:5 * j, 0:D], slots(bank[1], P, w=D), ACT.Copy).then_inc(s_root, 1)
            act.wait_ge(s_o5, T // 5)
            act.activation(H[:, T - 5:T, 0:D], slots(bank[1], P, w=D), ACT.Copy).then_inc(s_root, 1)
            act.wait_ge(s_parts, 2)
            act.activation(X3[:, :, 1, :], X1[:, :, :], ACT.Copy).then_inc(s_parts, 1)
            for n, (h, keys) in enumerate([(h, keys) for h in range(HALVES) for keys in (row_key, col_key)]):
                act.wait_ge(s_wkt, n + 1)
                act.activation(keys[:, :, h].rearrange("p (g j) -> p g j", g=G), slots(bank[n % 2], 128), ACT.Copy
                               ).then_inc(s_wks, 1)
            act.wait_ge(s_flag, 1)
            act.wait_ge(s_parts, 4)

            def main(fast):
                at, ar = (AT_b, AR_b) if fast else (AT, AR)

                def step(k, b, t):
                    for g in range(NG):
                        if has(t):
                            if g == 0:
                                ge(act, s_ai, t - 1)
                                ge(act, s_deg, t - 1)
                            ge(act, s_built, NG * t + g + 1)
                            w = GW * WN
                            act.activation(at[b][:, :, g * w:(g + 1) * w].rearrange("p h (w l) -> p w l h", l=WN),
                                           slots(BP, P).rearrange("p w (l h) -> p w l h", h=T), ACT.Copy
                                           ).then_inc(s_at, 1)
                        if has(t - 1):
                            if g == 0:
                                ge(act, s_out, NC * (t - 2))
                                ge(act, s_store[1 - b], 16 * (k - 1 + b))
                                if fast:
                                    act.activation(xt3[1 - b][:, :, :].rearrange("p i d -> p (i d)"),
                                                   X3f[:, cols(t - 1, 3 * D)], ACT.Copy).then_inc(s_x3, 1)
                            ge(act, s_tp, NG * (t - 1) + g + 1)
                            act.activation(ar[1 - b][:, g * 625:(g + 1) * 625].rearrange("p (k j) -> p k j", k=5),
                                           slots_b(TP) if fast else slots(TP, P), ACT.Copy,
                                           accum_out=deg_part[:, cols((t - 1) * NG + g, 1)]).then_inc(s_ar, 1)
                    if has(t - 1):
                        ge(act, s_ai, t)
                        act.activation(sums_in[:, cols(t - 1, P)], AI[:, 0:P], ACT.Copy).then_inc(s_agin, 1)
                steps(act, step, T)

            in_mode(act, main)

            for j in range(T // 5):
                act.wait_ge(s_y5T, j + 1)
                act.activation(x5T[:, :, :], slots(bank[3], D), ACT.Copy).then_inc(s_y5Ts, 1)
                act.wait_ge(s_h5, j + 1)
                act.activation(H[:, 5 * j:5 * j + 5, 0:D], slots(bank[2], P, w=D), ACT.Copy).then_inc(s_h5s, 1)
                act.activation(a_d[:, 5 * j:5 * j + 5], bank[2][0:P, 5 * D:5 * D + 5], ACT.Copy).then_inc(s_h5s, 1)
                act.wait_ge(s_arow, j + 1)
                act.activation(a_row[0:P, j * 5 * P:(j + 1) * 5 * P].rearrange("p (k i) -> p k i", k=5), slots(bank[3], P),
                               ACT.Copy).then_inc(s_arows, 1)

            def relu(t, b):
                act.wait_ge(s_m, t + 1)
                ge(act, s_e, t - 1)
                for c0, c1, s_done in ((LC, N, s_relup), (0, LC, s_relu)):
                    act.activation(R[b][:, c0:c1], S[b][:, c0:c1], ACT.Relu, bias=mx[b][:, 3:4], scale=(1.0 - SLOPE) / SLOPE
                                   ).then_inc(s_done, 1)

            def exp(t, b):
                act.wait_ge(s_lr, t + 1)
                act.wait_ge(s_lrp, t + 1)
                act.wait_ge(s_bias, t + 1)
                ge(act, s_t2, NG * (t - 1))
                act.activation(V2[b], R[b], ACT.Exp, bias=mx[b][:, 2:3], scale=SLOPE).then_inc(s_e, 1)

            def evict(t, g):
                act.wait_ge(s_t2, NG * t + g + 1)
                ge(act, s_mm, NG * (t - 1) + g + 1)
                act.activation(PT[g][:, :, :], slots(TSLOT[g], P), ACT.Copy).then_inc(s_ev, 1)

            relu(0, 0)
            exp(0, 0)
            relu(1, 1)

            def step2(k, b, t):
                if has(t + 1):
                    exp(t + 1, (b + 1) % 2)
                if has(t - 1):
                    evict(t - 1, 3)
                    evict(t - 1, 4)
                if has(t + 2):
                    relu(t + 2, b % 2)
                for g in range(3):
                    if has(t):
                        evict(t, g)
            steps(act, step2, T, 4)

        @block.vector
        def _(dve):
            chain = Chain(dve, s_chain)
            V = nc.vector

            def floor_div(value, q_out, rem_out, qi, neg, chain=chain):
                chain(V.tensor_scalar(qi, value, 0.5, 1.0 / P, ALU.add, ALU.mult))
                chain(V.tensor_copy(q_out, qi))
                chain(V.scalar_tensor_tensor(out=rem_out, in0=q_out, scalar=-float(P), in1=value,
                                             op0=ALU.mult, op1=ALU.add))
                chain(V.tensor_scalar(neg, rem_out, 0.0, None, ALU.is_lt))
                chain(V.tensor_tensor(q_out, q_out, neg, ALU.subtract))
                chain(V.scalar_tensor_tensor(out=rem_out, in0=neg, scalar=float(P), in1=rem_out,
                                             op0=ALU.mult, op1=ALU.add))

            dve.wait_ge(s_const, CONSTS)
            chain(V.tensor_copy(window[:, :], window_i[:, :]))
            chain(V.tensor_scalar(wbase, window[:, :], float(WN), None, ALU.mult))
            dve.wait_ge(s_ld["dst"], 16)
            chain(V.tensor_copy(cmp_f[:, 0:1], dst_i[:, 0:1]))
            V.tensor_scalar(heads, ident[0:P, 0:P], cmp_f[:, 0:1], None, ALU.mult).then_inc(s_hb0, 1)
            dve.wait_ge(s_ld["src"], 16)
            V.scalar_tensor_tensor(out=flat, in0=dst_i, scalar=float(N), in1=src_i,
                                   op0=ALU.mult, op1=ALU.add).then_inc(s_flatk, 1)
            dve.wait_ge(s_flatk, 1)
            dve.wait_ge(s_hb, 1)
            for g in range(G):
                chain(V.tensor_scalar(cmp_f[:, 0:P], AI[0:P, 0:P], wbase[:, g:g + 1], 0.0, ALU.is_lt, ALU.add,
                                      accum_out=krow[:, g:g + 1]))
            chain(V.tensor_scalar(rowno, krow, -1.0, 0.0, ALU.add, ALU.max))
            V.tensor_copy(rowno_i, rowno).then_inc(s_rowno, 1)
            dve.wait_ge(s_ld["rows"], 16 * 6)
            chain(V.tensor_copy(brow[:, 0:3, :], rows_in[:, 0:3, :]))
            chain(V.tensor_tensor(brow[:, 3, :], rows_in[:, 3, :], rows_in[:, 4, :], ALU.add))
            V.scalar_tensor_tensor(out=brow[:, 3, :], in0=brow[:, 3, :], scalar=0.5, in1=rows_in[:, 5, :],
                                   op0=ALU.mult, op1=ALU.add).then_inc(s_brow, 1)
            for h in range(HALVES):
                chain.add(V.tensor_copy(iota_b[:, :, h], iota_i[:, :]))
            chain.add(V.tensor_copy(iota_f[:, :], iota_i[:, :]))
            chain.add(V.tensor_copy(ident_b[:, :], ident[0:P, 0:P]))
            chain.add(V.tensor_copy(win_off[:, :], win_off_i))
            dve.wait_ge(s_wts, 1)
            V.tensor_tensor(WrT[:, :], WrT[:, :], ident[:, :], ALU.add).then_inc(s_wre, 1)
            for g in range(G):
                dve.wait_ge(s_cand[g], 16)
                chain(V.tensor_scalar(cmp_f, cand[g], wbase[:, g:g + 1], 0.0, ALU.is_lt, ALU.add,
                                      accum_out=krow[:, g:g + 1]))
            chain(V.scalar_tensor_tensor(out=start, in0=rowno, scalar=float(EC), in1=krow, op0=ALU.mult, op1=ALU.add))
            chain(V.tensor_copy(start_i, start))
            V.tensor_scalar(start_i, start_i, 5, None, ALU.arith_shift_right).then_inc(s_start, 1)
            dve.wait_ge(s_parts, 1)
            V.tensor_tensor(X1[:, :, :], X[:, :, :], X3[:, :, 0, :], ALU.subtract).then_inc(s_parts, 1)
            dve.wait_ge(s_bc, 2)
            V.tensor_copy(bc[:, :, :].rearrange("p k d -> p (k d)"), OP[0][0:P, :]).then_inc(s_bcs, 1)
            V.tensor_copy(bcD[:, :, :].rearrange("p k d -> p (k d)"), OP[1][:, 0:2 * D]).then_inc(s_bcs, 1)
            dve.wait_ge(s_bcs, 2)
            dve.wait_ge(s_ld["w"], 64)
            for i in range(2):
                chain(V.tensor_tensor(Wx[:, :], Wg[:, :], bcD[:, i, :], ALU.mult))
                chain(V.tensor_reduce(out=Wa[:, i:i + 1], in_=Wx[:, :], axis=AX, op=ALU.add))
            chain(V.tensor_copy(Wa_wide[:, :], Wa[:, 0:1].broadcast_to([D, P])))
            dve.wait_ge(s_win, 16 * G)
            chain(V.memset(win.rearrange("p (g c) -> p g c", c=CAP)[:, :, CAP - 1:CAP], -1.0e9))
            for g in range(G):
                chain(V.scalar_tensor_tensor(out=win[:, g * CAP:(g + 1) * CAP],
                                             in0=window[:, g:g + 1].broadcast_to([P, CAP]), scalar=-float(WSPAN),
                                             in1=win[:, g * CAP:(g + 1) * CAP], op0=ALU.mult, op1=ALU.add))
            floor_div(win, q_f, rem_f, q_i, neg_f)
            V.memset(tick[:, 7:8], 0.0).then_inc(s_wkeys, 1)
            chain(V.tensor_scalar(neg_f, q_f, 0.0, 0.0, ALU.is_ge, ALU.add, accum_out=c2[:, 0:1]))
            chain(V.tensor_scalar(neg_f, q_f, float(P), 0.0, ALU.is_ge, ALU.add, accum_out=c2[:, 1:2]))
            V.tensor_tensor(okc, c2[:, 0:1], c2[:, 1:2], ALU.subtract).then_inc(s_vsum, 1)
            V.memset(sums_out[:, :], 0.0).then_inc(s_acc, 1)
            dve.wait_ge(s_vtot, 1)
            chain(V.tensor_copy(total[:, :], OP[1][0:1, 0:1]))
            V.tensor_scalar(flag[:, :], total[:, :], float(E), None, ALU.is_equal).then_inc(s_flag, 1)
            dve.wait_ge(s_flag, 1)
            dve.wait_ge(s_wks, 2 * HALVES)
            dve.wait_ge(s_acc, 1)
            V.memset(tick[:, 5:6], 0.0).then_inc(s_ghot, 1)
            V.memset(tick[:, 6:7], 0.0).then_inc(s_ghotused, 1)

            def main(fast):
                def onehots(t, b, g):
                    n = NG * t + g
                    q = (b + g) % 2
                    if fast:
                        ge(dve, s_built, n - 1)
                        for keys, hot in ((row_key, row_hot), (col_key, col_hot)):
                            full = [128, GW, 128, HALVES]
                            ins = V.tensor_tensor(
                                hot[:, q, :, :, :], iota_b[:, :, :].rearrange("p (a k) h -> p a k h", a=1).broadcast_to(full),
                                keys[:, cols(n, GW), :].rearrange("p (w a) h -> p w a h", a=1).broadcast_to(full), ALU.is_equal)
                        ins.then_inc(s_hot, 1)
                    else:
                        with dve.Fori(0, GW) as w:
                            ge(dve, s_ghot, (n * GW + w) * NB + 1)
                            V.tensor_scalar(gen_key, all_row[:, :], win_off[:, bass.ds(n * GW + w, 1)], None,
                                            ALU.subtract).then_inc(s_gkey, 1)
                            ge(dve, s_gkey, n * GW + w + 1)
                            carry(0)
                            with dve.Fori(0, NB) as c:
                                ge(dve, s_ghotused, (n * GW + w) * NB + c + 1)
                                io = iota_f[0:P, 0:P].rearrange("p (a k) -> p a k", a=1).broadcast_to([P, GB, P])
                                V.tensor_tensor(gen_row, io, gen_key[:, bass.ds(c * GB, GB)].rearrange(
                                    "p (c a) -> p c a", a=1).broadcast_to([P, GB, P]), ALU.is_equal)
                                V.tensor_tensor(gen_col, io, all_col[:, bass.ds(c * GB, GB)].rearrange(
                                    "p (c a) -> p c a", a=1).broadcast_to([P, GB, P]), ALU.is_equal).then_inc(s_ghot, 1)

                if not fast:
                    decode = Chain(dve, s_gdec)
                    decode(V.tensor_copy(all_src, src_i))
                    floor_div(all_src, all_row[:, :], all_col[:, :], q_i[:, 0:EC], neg_f[:, 0:EC], decode)
                    decode(V.scalar_tensor_tensor(out=all_row[:, :], in0=dst_i, scalar=float(T), in1=all_row[:, :],
                                                  op0=ALU.mult, op1=ALU.add))
                onehots(0, 0, 0)

                def step(k, b, t):
                    for g in range(NG):
                        if g < NG - 1:
                            if has(t):
                                onehots(t, b, g + 1)
                        elif has(t + 1):
                            onehots(t + 1, 1 - b, 0)
                        if has(t - 2):
                            for c in CHUNK_AT[g]:
                                m = NC * (t - 2) + c
                                c0, w = CHUNKS[c]
                                ge(dve, s_acc, m)
                                ge(dve, s_out, m + 1)
                                V.tensor_tensor(sums_out[:, c0:c0 + w], sums_out[:, c0:c0 + w], OP[(NC * b + c) % 2][:, 0:w],
                                                ALU.add).then_inc(s_acc, 1)
                steps(dve, step, T + 1)

            in_mode(dve, main)

            tail = Chain(dve, s_chain, chain.n)
            dve.wait_ge(s_ar, NG * T)
            dve.wait_ge(s_deg, T)
            dve.wait_ge(s_acc, NC * T + 1)
            tail(V.tensor_reduce(out=deg_in[:, :], in_=deg_part[:, :].rearrange("p (t g) -> p t g", g=NG), axis=AX, op=ALU.add))
            tail(V.tensor_reduce(out=deg_out[:, :], in_=deg_sum, axis=AX, op=ALU.add))
            for d in (deg_in, deg_out):
                tail(V.tensor_scalar(d[:, :], d[:, :], 1.0, None, ALU.max))
                tail(V.reciprocal(d[:, :], d[:, :]))

            def self_loops(fast, n, b, t):
                i, a = (b, AR_b[b]) if fast else (0, AR[0])
                dve.wait_ge(s_load[i], 16 * (n + 1))
                V.tensor_tensor(a[:, cols(t, P)], a[:, cols(t, P)], ident[0:P, 0:P], ALU.add).then_inc(s_self, 1)

            def mask(fast, b, t):
                a = AR_b[b] if fast else AR[0]
                dve.wait_ge(s_self, t + 1)
                V.tensor_scalar(pen[b % 2], a[:, :], 0.0, -NEG, ALU.is_equal, ALU.mult).then_inc(s_pen, 1)

            def first_masks(fast):
                for t in range(2):
                    self_loops(fast, 0 if fast else t, t, t)
                    mask(fast, t, t)

            dve.wait_ge(s_hbias, 1)
            for j in range(T // 5):
                if j == 1:
                    in_mode(dve, first_masks)
                dve.wait_ge(s_mean5, j + 1)
                for i in range(5):
                    t = 5 * j + i
                    tail.add(V.scalar_tensor_tensor(out=X1[:, t, :], in0=bank[0][0:P, i * D:(i + 1) * D],
                                                    scalar=deg_in[:, t:t + 1], in1=H[:, t, 0:D],
                                                    op0=ALU.mult, op1=ALU.add))
                tail.wait()
                for i in range(5):
                    t = 5 * j + i
                    ins = V.scalar_tensor_tensor(out=X1[:, t, :], in0=bank[1][0:P, i * D:(i + 1) * D],
                                                 scalar=deg_out[:, t:t + 1], in1=X1[:, t, :],
                                                 op0=ALU.mult, op1=ALU.add)
                ins.then_inc(s_sum5, 1)
                dve.wait_ge(s_sum5, j + 1)
                for i in range(5):
                    tail.add(V.bn_stats(st6[:, i, :], X1[:, 5 * j + i, :]))
                tail.wait()
                for i in range(5):
                    tail.add(V.bn_aggr(mv[:, i, :], st6[:, i, :]))
                tail.wait()
                V.tensor_scalar(ve5[:, :], mv[:, :, 1], EPS, None, ALU.add).then_inc(s_ve5, 1)
                dve.wait_ge(s_rs5, j + 1)
                for i in range(5):
                    ins = V.tensor_scalar(X1[:, 5 * j + i, :], X1[:, 5 * j + i, :], mv[:, i, 0:1], rstd[:, i:i + 1],
                                          ALU.subtract, ALU.mult)
                ins.then_inc(s_y5, 1)
            dve.wait_ge(s_y5, T // 5)
            dve.wait_ge(s_h5s, 2 * (T // 5))
            tail(V.tensor_scalar(slope_ad[:, :], a_d[:, :], SLOPE, None, ALU.mult))
            tail(V.tensor_scalar(relu_ad[:, :], a_d[:, :], (1.0 - SLOPE) / SLOPE, None, ALU.mult))
            dve.wait_ge(s_arows, T // 5)
            dve.wait_ge(s_x1b, 1)

            BS = 2
            FS = 5

            def row_max(t, b):
                ge(dve, s_lr, t - 1)
                ge(dve, s_lrp, t - 1)
                V.tensor_copy(mx[b][:, 3:4], relu_ad[:, cols(t, 1)])
                dve.wait_ge(s_pen, t + 1)
                carry(2 + b)
                V.tensor_tensor_reduce(out=S[b][:, :], in0=a_row[0:P, :], in1=pen[b], scale=1.0, scalar=NEG,
                                       op0=ALU.subtract, op1=ALU.max, accum_out=mx[b][:, 0:1]).then_inc(s_m, 1)

            def exp_bias(t, b, i):
                if i == 0:
                    dve.wait_ge(s_m, t + 1)
                    ge(dve, s_e, t - 1)
                else:
                    dve.wait_ge(s_c2, t * BS + i)
                if i == 0:
                    ins = V.tensor_tensor(mx[b][:, 1:2], mx[b][:, 0:1], a_d[:, cols(t, 1)], ALU.add)
                elif i == 1:
                    ins = V.scalar_tensor_tensor(out=mx[b][:, 2:3], in0=mx[b][:, 1:2], scalar=SLOPE, in1=mx[b][:, 1:2],
                                                 op0=ALU.mult, op1=ALU.max)
                else:
                    ins = V.tensor_tensor(mx[b][:, 2:3], slope_ad[:, cols(t, 1)], mx[b][:, 2:3], ALU.subtract)
                ins.then_inc(s_bias if i == BS else s_c2, 1)

            def leaky(t, b):
                dve.wait_ge(s_relu, t + 1)
                V.tensor_tensor(R[b][:, 0:LC], S[b][:, 0:LC], R[b][:, 0:LC], ALU.add).then_inc(s_lr, 1)

            def finish(k, b, t, i):
                o = OP[b]
                if i == 0:
                    dve.wait_ge(s_mm, NG * (t + 1))
                    ge(dve, s_res[b], 16 * k)
                else:
                    dve.wait_ge(s_f2, t * FS + i)
                if i == 0:
                    ins = V.tensor_scalar(rden[b][:, :], o[0:P, D:D + 1], 1e-16, None, ALU.add)
                elif i == 1:
                    ins = V.reciprocal(rden[b][:, :], rden[b][:, :])
                elif i == 2:
                    ins = V.scalar_tensor_tensor(out=fin[b][:, :], in0=o[0:P, 0:D], scalar=rden[b][:, 0:1],
                                                 in1=X1f[:, cols(t, D)], op0=ALU.mult, op1=ALU.add)
                elif i == 3:
                    ins = V.bn_stats(st2[b][:, :], fin[b][:, :])
                elif i == 4:
                    carry(4 + b)
                    ins = V.bn_aggr(mv2[b][:, :], st2[b][:, :])
                else:
                    ins = V.tensor_scalar(ve2[b][:, :], mv2[b][:, 1:2], EPS, None, ALU.add)
                ins.then_inc(s_ve2 if i == FS else s_f2, 1)

            def normalize(t, b):
                dve.wait_ge(s_rs2, t + 1)
                V.tensor_scalar(fin[b][:, :], fin[b][:, :], mv2[b][:, 0:1], rs2[b][:, 0:1],
                                ALU.subtract, ALU.mult).then_inc(s_fin, 1)

            def layer2(fast):
                def weights(t, b):
                    a, v = AR_b[b] if fast else AR[1], V2[b % 2]
                    if not fast:
                        dve.wait_ge(s_load[1], 16 * (t + 1))
                        V.tensor_tensor(a[:, cols(t, P)], a[:, cols(t, P)], ident[0:P, 0:P], ALU.add).then_inc(s_wself, 1)
                        dve.wait_ge(s_wself, t + 1)
                        carry(0)
                    dve.wait_ge(s_e, t + 1)
                    V.tensor_tensor(v[:, 0:HALF], v[:, 0:HALF], a[:, 0:HALF], ALU.mult).then_inc(s_p, 1)

                def bias(t, b):
                    for i in range(BS + 1):
                        exp_bias(t, b, i)

                row_max(0, 0)
                bias(0, 0)
                row_max(1, 1)
                bias(1, 1)
                leaky(0, 0)
                self_loops(fast, 0 if fast else 2, 2, 2)
                mask(fast, 2, 2)
                row_max(2, 0)
                bias(2, 0)
                weights(0, 0)
                leaky(1, 1)

                def step2(k, b, t):
                    def last_result(i):
                        if has(t - 2):
                            finish(nth(k, b, -2, 2), b % 2, t - 2, i)

                    def next_bias(i):
                        if has(t + 3):
                            exp_bias(t + 3, (b + 3) % 2, i)

                    last_result(0)
                    if has(t - 3):
                        normalize(t - 3, (b + 1) % 2)
                    last_result(1)
                    if has(t + 3):
                        self_loops(fast, nth(k, b, 3, 4) if fast else t + 3, (b + 3) % 4, t + 3)
                    last_result(2)
                    if has(t + 3):
                        mask(fast, (b + 3) % 4, t + 3)
                    last_result(3)
                    if has(t + 3):
                        row_max(t + 3, (b + 3) % 2)
                    last_result(4)
                    next_bias(0)
                    last_result(5)
                    next_bias(1)
                    if has(t + 1):
                        weights(t + 1, (b + 1) % 4)
                    next_bias(2)
                    if has(t + 2):
                        leaky(t + 2, b % 2)
                steps(dve, step2, T + 2, 4)

            in_mode(dve, layer2)

        @block.tensor
        def _(pe):
            M = nc.tensor
            pe.wait_ge(s_hb0, 1)
            M.matmul(AI[0:P, 0:P], ones[:, :], heads, start=True, stop=True).then_inc(s_hb, 1)
            pe.wait_ge(s_ld["w"], 64)
            pe.wait_ge(s_rowno, 1)
            for k in range(3):
                ins = M.transpose(AI[:, k * D:(k + 1) * D], Wst[k][:, :], ident[:, :])
            ins.then_inc(s_wt, 1)
            pe.wait_ge(s_brow, 1)
            M.matmul(OP[0][0:P, :], ones_row[:, 0:P], brow[:, :, :].rearrange("p k d -> p (k d)"), start=True, stop=True
                     ).then_inc(s_bc, 1)
            M.matmul(OP[1][:, 0:2 * D], ones_row[:, :], brow[:, 0:2, :].rearrange("p k d -> p (k d)"), start=True, stop=True
                     ).then_inc(s_bc, 1)
            pe.wait_ge(s_ld["x"], 16)
            pe.wait_ge(s_wre, 1)
            def root_transposes(j):
                if j:
                    pe.wait_ge(s_x5Ts, j)
                for i in range(5):
                    ins = M.transpose(bank[0][:, i * 128:i * 128 + P], X[:, 5 * j + i, :], ident[0:P, 0:P])
                ins.then_inc(s_x5T, 1)

            root_transposes(0)
            for j in range(T // 5):
                if j + 1 < T // 5:
                    root_transposes(j + 1)
                pe.wait_ge(s_x5Ts, j + 1)
                if j:
                    pe.wait_ge(s_root, j)
                for i in range(5):
                    ins = M.matmul(bank[1][0:P, i * D:(i + 1) * D], x5T[:, i, :], WrT[:, :], start=True, stop=True)
                ins.then_inc(s_o5, 1)
            pe.wait_ge(s_root, T // 5)
            pe.wait_ge(s_wkeys, 1)
            for n, (h, keys) in enumerate([(h, keys) for h in range(HALVES) for keys in (q_f, rem_f)]):
                if n >= 2:
                    pe.wait_ge(s_wks, n - 1)
                for g in range(G):
                    ins = M.transpose(bank[n % 2][:, g * 128:g * 128 + P],
                                      keys[:, g * CAP + h * 128:g * CAP + (h + 1) * 128], ident[0:P, 0:P])
                ins.then_inc(s_wkt, 1)
                if n == 1:
                    pe.wait_ge(s_bcs, 2)
                    pe.wait_ge(s_vsum, 1)
                    M.matmul(OP[1][0:1, 0:1], okc, ones[:, 0:1], start=True, stop=True).then_inc(s_vtot, 1)
            pe.wait_ge(s_wks, 2 * HALVES)
            pe.wait_ge(s_wts, 3)
            pe.wait_ge(s_flag, 1)
            pe.wait_ge(s_parts, 4)

            def main(fast):
                def step(k, b, t):
                    for g in range(NG):
                        if has(t):
                            n = NG * t + g
                            q = (b + g) % 2
                            ge(pe, s_at, n)
                            if fast:
                                ge(pe, s_hot, n + 1)
                                for w in range(GW):
                                    for h in range(HALVES):
                                        ins = M.matmul(BP[:, w * 128:w * 128 + P], col_hot[:, q, w, :, h], row_hot[:, q, w, 0:P, h],
                                                       start=(h == 0), stop=(h == HALVES - 1))
                                ins.then_inc(s_built, 1)
                            else:
                                M.matmul(OPX, zero_w[:, 0:1], zero_w[:, 0:1], start=True, stop=True)
                                with pe.Fori(0, GW) as w:
                                    o = BP[0:P, bass.ds(w * 128, P)]
                                    M.matmul(o, zero_w[:, :], zero_w[:, :], start=True, stop=False)
                                    with pe.Fori(0, NB) as c:
                                        ge(pe, s_ghot, (n * GW + w) * NB + c + 2)
                                        for e in range(GB):
                                            ins = M.matmul(o, gen_col[:, e, :], gen_row[:, e, :], start=False, stop=False)
                                        ins.then_inc(s_ghotused, 1)
                                    M.matmul(o, zero_w[:, :], zero_w[:, :], start=False, stop=True)
                                M.matmul(OPX, zero_w[:, 0:1], zero_w[:, 0:1], start=True, stop=True).then_inc(s_built, 1)
                        if has(t - 1):
                            u = NG * (t - 1) + g
                            a = AT_b[1 - b] if fast else AT[1 - b]
                            ge(pe, s_at, NG * t)
                            ge(pe, s_ar, u)
                            for i in range(5):
                                if fast:
                                    ins = M.transpose(slots_b(TP)[:, i, :], a[:, 5 * g + i, :], ident_b[:, :])
                                else:
                                    ins = M.transpose(TP[0:P, i * 128:i * 128 + P], a[:, 5 * g + i, :], ident[0:P, 0:P])
                            ins.then_inc(s_tp, 1)
                            if g == 0:
                                ge(pe, s_agin, t - 1)
                            for i in range(5):
                                h = 5 * g + i
                                for j in range(3 if fast else 1):
                                    ins = M.matmul(AI[:, 0:P], X3[:, h, j, :] if fast else X[:, h, :], a[:, h, :],
                                                   start=(h == 0 and j == 0), stop=(h == T - 1 and j == (2 if fast else 0)))
                            if g == NG - 1:
                                ins.then_inc(s_ai, 1)
                        if has(t - 2):
                            if g == 0:
                                ge(pe, s_ar, NG * (t - 1))
                                if fast:
                                    ge(pe, s_x3, t - 1)
                                else:
                                    pe.wait_ge(s_xt[b], 16 * k)
                            for c in CHUNK_AT[g]:
                                c0, w = CHUNKS[c]
                                ge(pe, s_acc, NC * (t - 2) + c)
                                for j in range(3 if fast else 1):
                                    ins = M.matmul(OP[(NC * b + c) % 2][:, 0:w], xt3[b][:, j, :] if fast else xt[b][:, :],
                                                   (AR_b if fast else AR)[b][:, c0:c0 + w],
                                                   start=(j == 0), stop=(j == (2 if fast else 0)))
                                ins.then_inc(s_out, 1)
                steps(pe, step, T + 1)

            in_mode(pe, main)

            pe.wait_ge(s_acc, NC * T + 1)
            pe.wait_ge(s_agin, T)
            def means(j):
                if j:
                    pe.wait_ge(s_sum5, j)
                for i in range(5):
                    t = 5 * j + i
                    M.matmul(bank[0][0:P, i * D:(i + 1) * D], sums_in[:, t * P:(t + 1) * P], WiT[:, :], start=True, stop=True)
                    ins = M.matmul(bank[1][0:P, i * D:(i + 1) * D], sums_out[:, t * P:(t + 1) * P], WoT[:, :],
                                   start=True, stop=True)
                ins.then_inc(s_mean5, 1)

            means(0)
            for j in range(T // 5):
                if j + 1 < T // 5:
                    means(j + 1)
                pe.wait_ge(s_y5, j + 1)
                if j:
                    pe.wait_ge(s_arows, j)
                for i in range(5):
                    ins = M.transpose(bank[3][:, i * 128:i * 128 + P], X1[:, 5 * j + i, :], ident[0:P, 0:P])
                ins.then_inc(s_y5T, 1)
                pe.wait_ge(s_y5Ts, j + 1)
                if j:
                    pe.wait_ge(s_h5s, 2 * j)
                for i in range(5):
                    M.matmul(bank[2][0:P, i * D:(i + 1) * D], x5T[:, i, :], Wg[:, :], start=True, stop=True)
                    ins = M.matmul(bank[2][0:P, 5 * D + i:5 * D + i + 1], x5T[:, i, :], Wa[:, 1:2], start=True, stop=True)
                ins.then_inc(s_h5, 1)
                for i0, i1 in ((0, 4), (4, 5)):
                    ins = M.matmul(slots(bank[3], P)[:, i0:i1, :], Wa_wide[:, :], x5T[:, i0:i1, :], start=True, stop=True)
                ins.then_inc(s_arow, 1)
            pe.wait_ge(s_h5s, 2 * (T // 5))

            pe.wait_ge(s_arows, T // 5)

            def transposes(t, b, g):
                if g == 0:
                    pe.wait_ge(s_p, t + 1)
                if g == HALF // 625:
                    pe.wait_ge(s_pp, t + 1)
                n = {0: NG * t - 1, 1: NG * t, 2: NG * t - 2, 3: NG * t + 1, 4: NG * t + 2}[g]
                ge(pe, s_ev, n)
                for i in range(5):
                    h = 5 * g + i
                    ins = M.transpose(TSLOT[g][0:P, i * 128:i * 128 + P], V2[b][:, h * P:(h + 1) * P], ident[0:P, 0:P])
                ins.then_inc(s_t2, 1)

            transposes(0, 0, 0)
            transposes(0, 0, 1)

            def step2(k, b, t):
                for g in range(NG):
                    for n in ((2, 3, 4), (), (), (), ())[g]:
                        transposes(t, b, n)
                    if g >= 3 and has(t + 1):
                        transposes(t + 1, 1 - b, g - 3)
                    if g == 0:
                        ge(pe, s_ve2, t - 1)
                    pe.wait_ge(s_ev, NG * t + g + 1)
                    for i in range(5):
                        h = 5 * g + i
                        ins = M.matmul(OP[b][0:P, 0:D + 1], PT[g][:, i, :], H[:, h, :],
                                       start=(h == 0), stop=(h == T - 1))
                    ins.then_inc(s_mm, 1)
            steps(pe, step2, T - 1)


_INS = ["x", "src", "dst", "L0_gnn_W_in", "L0_gnn_b_in", "L0_gnn_W_out", "L0_gnn_b_out", "L0_gnn_W_root",
        "L0_gnn_b_root", "L1_gnn_W", "L1_gnn_att_src", "L1_gnn_att_dst", "L1_gnn_bias"]


def kernel(**inputs):
    import numpy as _np
    import concourse.bacc as _bacc
    from concourse import mybir as _mybir
    from concourse.bass_utils import run_bass_kernel_spmd as _run

    nc = _bacc.Bacc("TRN2", target_bir_lowering=False, num_devices=1)
    arrays, args = {}, []
    for name in _INS:
        a = _np.ascontiguousarray(inputs[name])
        arrays[f"in_{name}_dram"] = a
        args.append(nc.dram_tensor(f"in_{name}_dram", a.shape, _mybir.dt.from_np(a.dtype), kind="ExternalInput").ap())
    args.append(nc.dram_tensor("out_dram", tuple(inputs["x"].shape), _mybir.dt.float32, kind="ExternalOutput").ap())
    x, src, dst, W_in, b_in, W_out, b_out, W_root, b_root, W_gat, att_src, att_dst, b_gat, out = args
    gnn_resnorm_kernel(nc, x, src, dst, W_in, b_in, W_out, b_out, W_root, b_root, W_gat, att_src, att_dst,
                       b_gat, out)
    r = _run(nc, [arrays], core_ids=[0])
    return r.results[0]["out_dram"]
```
